# Optimizing a Trainium2 kernel written in Bass

```python
import numpy as np
import jax
import jax.numpy as jnp

def _softmax(x, axis=-1):
    return jax.nn.softmax(x, axis=axis)

def _gelu(x):
    return jax.nn.gelu(x, approximate=True)

def _silu(x):
    return jax.nn.silu(x)

def _sigmoid(x):
    return jax.nn.sigmoid(x)

def _layernorm(x, axis=-1, eps=1e-05):
    m = jnp.mean(x, axis=axis, keepdims=True)
    v = jnp.var(x, axis=axis, keepdims=True)
    return (x - m) / jnp.sqrt(v + eps)

def _scatter_add(tgt, idx, src, axis=0):
    return tgt.at[idx].add(src)

def _segment_sum(src, seg, n):
    return jax.ops.segment_sum(src, seg, n)
kernel_name = 'mk_dlrm_tower_d1_rec_r8_0ae9fb'

def setup_inputs(seed: int=0):
    np.random.seed(seed)
    _w = jnp.asarray

    def _rec_inputs():
        import jax
        import jax.numpy as jnp
        _tk = jax.random.key(seed)
        dense_ctx = jax.random.normal(jax.random.fold_in(_tk, 190), (1024, 16), jnp.float32)
        ids = jnp.stack([jax.random.randint(jax.random.fold_in(_tk, 200 + f), (1024,), 0, v, jnp.int32) for f, v in enumerate([12500, 12500, 1000, 1000, 12500, 1250, 125000, 1250, 1250, 12500, 1250, 125000, 125000, 1000, 12500, 1250, 1000, 12500, 1000, 1250, 12500, 125000, 1000, 1000, 125000, 1250, 125000, 125000, 1000, 12500, 12500, 12500, 1000, 125000, 12500, 1000, 12500, 12500, 12500])], axis=1)
        tbl_0 = 0.05 * jax.random.normal(jax.random.fold_in(_tk, 500 + 0), (12500, 16), jnp.float32)
        tbl_1 = 0.05 * jax.random.normal(jax.random.fold_in(_tk, 500 + 1), (12500, 16), jnp.float32)
        tbl_2 = 0.05 * jax.random.normal(jax.random.fold_in(_tk, 500 + 2), (1000, 16), jnp.float32)
        tbl_3 = 0.05 * jax.random.normal(jax.random.fold_in(_tk, 500 + 3), (1000, 16), jnp.float32)
        tbl_4 = 0.05 * jax.random.normal(jax.random.fold_in(_tk, 500 + 4), (12500, 16), jnp.float32)
        tbl_5 = 0.05 * jax.random.normal(jax.random.fold_in(_tk, 500 + 5), (1250, 16), jnp.float32)
        tbl_6 = 0.05 * jax.random.normal(jax.random.fold_in(_tk, 500 + 6), (125000, 16), jnp.float32)
        tbl_7 = 0.05 * jax.random.normal(jax.random.fold_in(_tk, 500 + 7), (1250, 16), jnp.float32)
        tbl_8 = 0.05 * jax.random.normal(jax.random.fold_in(_tk, 500 + 8), (1250, 16), jnp.float32)
        tbl_9 = 0.05 * jax.random.normal(jax.random.fold_in(_tk, 500 + 9), (12500, 16), jnp.float32)
        tbl_10 = 0.05 * jax.random.normal(jax.random.fold_in(_tk, 500 + 10), (1250, 16), jnp.float32)
        tbl_11 = 0.05 * jax.random.normal(jax.random.fold_in(_tk, 500 + 11), (125000, 16), jnp.float32)
        tbl_12 = 0.05 * jax.random.normal(jax.random.fold_in(_tk, 500 + 12), (125000, 16), jnp.float32)
        tbl_13 = 0.05 * jax.random.normal(jax.random.fold_in(_tk, 500 + 13), (1000, 16), jnp.float32)
        tbl_14 = 0.05 * jax.random.normal(jax.random.fold_in(_tk, 500 + 14), (12500, 16), jnp.float32)
        tbl_15 = 0.05 * jax.random.normal(jax.random.fold_in(_tk, 500 + 15), (1250, 16), jnp.float32)
        tbl_16 = 0.05 * jax.random.normal(jax.random.fold_in(_tk, 500 + 16), (1000, 16), jnp.float32)
        tbl_17 = 0.05 * jax.random.normal(jax.random.fold_in(_tk, 500 + 17), (12500, 16), jnp.float32)
        tbl_18 = 0.05 * jax.random.normal(jax.random.fold_in(_tk, 500 + 18), (1000, 16), jnp.float32)
        tbl_19 = 0.05 * jax.random.normal(jax.random.fold_in(_tk, 500 + 19), (1250, 16), jnp.float32)
        tbl_20 = 0.05 * jax.random.normal(jax.random.fold_in(_tk, 500 + 20), (12500, 16), jnp.float32)
        tbl_21 = 0.05 * jax.random.normal(jax.random.fold_in(_tk, 500 + 21), (125000, 16), jnp.float32)
        tbl_22 = 0.05 * jax.random.normal(jax.random.fold_in(_tk, 500 + 22), (1000, 16), jnp.float32)
        tbl_23 = 0.05 * jax.random.normal(jax.random.fold_in(_tk, 500 + 23), (1000, 16), jnp.float32)
        tbl_24 = 0.05 * jax.random.normal(jax.random.fold_in(_tk, 500 + 24), (125000, 16), jnp.float32)
        tbl_25 = 0.05 * jax.random.normal(jax.random.fold_in(_tk, 500 + 25), (1250, 16), jnp.float32)
        tbl_26 = 0.05 * jax.random.normal(jax.random.fold_in(_tk, 500 + 26), (125000, 16), jnp.float32)
        tbl_27 = 0.05 * jax.random.normal(jax.random.fold_in(_tk, 500 + 27), (125000, 16), jnp.float32)
        tbl_28 = 0.05 * jax.random.normal(jax.random.fold_in(_tk, 500 + 28), (1000, 16), jnp.float32)
        tbl_29 = 0.05 * jax.random.normal(jax.random.fold_in(_tk, 500 + 29), (12500, 16), jnp.float32)
        tbl_30 = 0.05 * jax.random.normal(jax.random.fold_in(_tk, 500 + 30), (12500, 16), jnp.float32)
        tbl_31 = 0.05 * jax.random.normal(jax.random.fold_in(_tk, 500 + 31), (12500, 16), jnp.float32)
        tbl_32 = 0.05 * jax.random.normal(jax.random.fold_in(_tk, 500 + 32), (1000, 16), jnp.float32)
        tbl_33 = 0.05 * jax.random.normal(jax.random.fold_in(_tk, 500 + 33), (125000, 16), jnp.float32)
        tbl_34 = 0.05 * jax.random.normal(jax.random.fold_in(_tk, 500 + 34), (12500, 16), jnp.float32)
        tbl_35 = 0.05 * jax.random.normal(jax.random.fold_in(_tk, 500 + 35), (1000, 16), jnp.float32)
        tbl_36 = 0.05 * jax.random.normal(jax.random.fold_in(_tk, 500 + 36), (12500, 16), jnp.float32)
        tbl_37 = 0.05 * jax.random.normal(jax.random.fold_in(_tk, 500 + 37), (12500, 16), jnp.float32)
        tbl_38 = 0.05 * jax.random.normal(jax.random.fold_in(_tk, 500 + 38), (12500, 16), jnp.float32)
        _rk = jax.random.fold_in(_tk, 7)
        W_top1 = 0.05 * jax.random.normal(jax.random.fold_in(_tk, 801), (400, 512), jnp.float32)
        W_top2 = 0.0441942 * jax.random.normal(jax.random.fold_in(_tk, 802), (512, 256), jnp.float32)
        W_top3 = 0.0625 * jax.random.normal(jax.random.fold_in(_tk, 803), (256, 1), jnp.float32)
        b_top1 = jnp.zeros((512,), jnp.float32)
        b_top2 = jnp.zeros((256,), jnp.float32)
        return (dense_ctx, ids, tbl_0, tbl_1, tbl_2, tbl_3, tbl_4, tbl_5, tbl_6, tbl_7, tbl_8, tbl_9, tbl_10, tbl_11, tbl_12, tbl_13, tbl_14, tbl_15, tbl_16, tbl_17, tbl_18, tbl_19, tbl_20, tbl_21, tbl_22, tbl_23, tbl_24, tbl_25, tbl_26, tbl_27, tbl_28, tbl_29, tbl_30, tbl_31, tbl_32, tbl_33, tbl_34, tbl_35, tbl_36, tbl_37, tbl_38, W_top1, b_top1, W_top2, b_top2, W_top3)
    dense_ctx, ids, tbl_0, tbl_1, tbl_2, tbl_3, tbl_4, tbl_5, tbl_6, tbl_7, tbl_8, tbl_9, tbl_10, tbl_11, tbl_12, tbl_13, tbl_14, tbl_15, tbl_16, tbl_17, tbl_18, tbl_19, tbl_20, tbl_21, tbl_22, tbl_23, tbl_24, tbl_25, tbl_26, tbl_27, tbl_28, tbl_29, tbl_30, tbl_31, tbl_32, tbl_33, tbl_34, tbl_35, tbl_36, tbl_37, tbl_38, W_top1, b_top1, W_top2, b_top2, W_top3 = _rec_inputs()

    def _L0_rec_setup():
        import jax, jax.numpy as jnp
        import numpy as np
        B, F0, D = (512, 39, 16)
        CIN = [128, 128, 128]

        def _cin_layer(X0, Xi, W, b):
            H = W.shape[0]
            F0_, Fi = (X0.shape[1], Xi.shape[1])
            Wr = W.reshape(H, F0_, Fi)
            return jnp.einsum('hjk,bjd,bkd->bhd', Wr, X0, Xi) + b[None, :, None]
        key = jax.random.key(seed)
        ks = jax.random.split(key, 4)
        x = jax.random.normal(ks[0], (B, F0, D), dtype=jnp.float32)
        fields = [F0] + CIN
        inp = {'embedded_features': x}
        for i in range(len(CIN)):
            cin = F0 * fields[i]
            cout = fields[i + 1]
            kw = jax.random.fold_in(ks[1], i)
            inp[f'W{i}'] = jax.random.normal(kw, (cout, cin), dtype=jnp.float32) / np.sqrt(cin)
            inp[f'b{i}'] = jnp.zeros((cout,), dtype=jnp.float32)
        return inp
    _L0_rec_all = _L0_rec_setup()
    _L0_rec_in = {k: v for k, v in _L0_rec_all.items() if k in ('W0', 'b0', 'W1', 'b1', 'W2', 'b2')}
    del _L0_rec_all
    return {'dense_ctx': dense_ctx, 'ids': ids, 'tbl_0': tbl_0, 'tbl_1': tbl_1, 'tbl_2': tbl_2, 'tbl_3': tbl_3, 'tbl_4': tbl_4, 'tbl_5': tbl_5, 'tbl_6': tbl_6, 'tbl_7': tbl_7, 'tbl_8': tbl_8, 'tbl_9': tbl_9, 'tbl_10': tbl_10, 'tbl_11': tbl_11, 'tbl_12': tbl_12, 'tbl_13': tbl_13, 'tbl_14': tbl_14, 'tbl_15': tbl_15, 'tbl_16': tbl_16, 'tbl_17': tbl_17, 'tbl_18': tbl_18, 'tbl_19': tbl_19, 'tbl_20': tbl_20, 'tbl_21': tbl_21, 'tbl_22': tbl_22, 'tbl_23': tbl_23, 'tbl_24': tbl_24, 'tbl_25': tbl_25, 'tbl_26': tbl_26, 'tbl_27': tbl_27, 'tbl_28': tbl_28, 'tbl_29': tbl_29, 'tbl_30': tbl_30, 'tbl_31': tbl_31, 'tbl_32': tbl_32, 'tbl_33': tbl_33, 'tbl_34': tbl_34, 'tbl_35': tbl_35, 'tbl_36': tbl_36, 'tbl_37': tbl_37, 'tbl_38': tbl_38, 'W_top1': W_top1, 'b_top1': b_top1, 'W_top2': W_top2, 'b_top2': b_top2, 'W_top3': W_top3, 'L0_rec_W0': _L0_rec_in['W0'], 'L0_rec_b0': _L0_rec_in['b0'], 'L0_rec_W1': _L0_rec_in['W1'], 'L0_rec_b1': _L0_rec_in['b1'], 'L0_rec_W2': _L0_rec_in['W2'], 'L0_rec_b2': _L0_rec_in['b2']}

def reference(dense_ctx, ids, tbl_0, tbl_1, tbl_2, tbl_3, tbl_4, tbl_5, tbl_6, tbl_7, tbl_8, tbl_9, tbl_10, tbl_11, tbl_12, tbl_13, tbl_14, tbl_15, tbl_16, tbl_17, tbl_18, tbl_19, tbl_20, tbl_21, tbl_22, tbl_23, tbl_24, tbl_25, tbl_26, tbl_27, tbl_28, tbl_29, tbl_30, tbl_31, tbl_32, tbl_33, tbl_34, tbl_35, tbl_36, tbl_37, tbl_38, W_top1, b_top1, W_top2, b_top2, W_top3, L0_rec_W0, L0_rec_b0, L0_rec_W1, L0_rec_b1, L0_rec_W2, L0_rec_b2):
    import jax
    import jax.numpy as jnp

    def _L0_rec_ref(embedded_features, W0, b0, W1, b1, W2, b2):
        import jax, jax.numpy as jnp
        import numpy as np
        B, F0, D = (512, 39, 16)
        CIN = [128, 128, 128]

        def _cin_layer(X0, Xi, W, b):
            H = W.shape[0]
            F0_, Fi = (X0.shape[1], Xi.shape[1])
            Wr = W.reshape(H, F0_, Fi)
            return jnp.einsum('hjk,bjd,bkd->bhd', Wr, X0, Xi) + b[None, :, None]
        X0 = embedded_features
        Ws = [(W0, b0), (W1, b1), (W2, b2)]
        Xi = X0
        res = []
        for W, b in Ws:
            Xi = _cin_layer(X0, Xi, W, b)
            res.append(Xi.sum(axis=2))
        return jnp.concatenate(res, axis=1)
    e = jnp.stack([tbl_0[ids[:, 0]], tbl_1[ids[:, 1]], tbl_2[ids[:, 2]], tbl_3[ids[:, 3]], tbl_4[ids[:, 4]], tbl_5[ids[:, 5]], tbl_6[ids[:, 6]], tbl_7[ids[:, 7]], tbl_8[ids[:, 8]], tbl_9[ids[:, 9]], tbl_10[ids[:, 10]], tbl_11[ids[:, 11]], tbl_12[ids[:, 12]], tbl_13[ids[:, 13]], tbl_14[ids[:, 14]], tbl_15[ids[:, 15]], tbl_16[ids[:, 16]], tbl_17[ids[:, 17]], tbl_18[ids[:, 18]], tbl_19[ids[:, 19]], tbl_20[ids[:, 20]], tbl_21[ids[:, 21]], tbl_22[ids[:, 22]], tbl_23[ids[:, 23]], tbl_24[ids[:, 24]], tbl_25[ids[:, 25]], tbl_26[ids[:, 26]], tbl_27[ids[:, 27]], tbl_28[ids[:, 28]], tbl_29[ids[:, 29]], tbl_30[ids[:, 30]], tbl_31[ids[:, 31]], tbl_32[ids[:, 32]], tbl_33[ids[:, 33]], tbl_34[ids[:, 34]], tbl_35[ids[:, 35]], tbl_36[ids[:, 36]], tbl_37[ids[:, 37]], tbl_38[ids[:, 38]]], axis=1)
    z = _L0_rec_ref(e, L0_rec_W0, L0_rec_b0, L0_rec_W1, L0_rec_b1, L0_rec_W2, L0_rec_b2)
    z = z.reshape(z.shape[0], -1)
    h = jnp.concatenate([z, dense_ctx], axis=1)
    h = jnp.maximum(h @ W_top1 + b_top1, 0.0)
    h = jnp.maximum(h @ W_top2 + b_top2, 0.0)
    y = h @ W_top3
    return y

_drawn_inputs = setup_inputs


def setup_inputs(seed=0):
    import zlib

    import numpy as np

    out = dict(_drawn_inputs(seed))
    spreads = {'b_top1': (0.0, 0.1),
     'b_top2': (0.0, 0.1),
     'L0_rec_b0': (0.0, 0.1),
     'L0_rec_b1': (0.0, 0.1),
     'L0_rec_b2': (0.0, 0.1)}
    factors = {'tbl_0': 8.0,
     'tbl_1': 5.963,
     'tbl_2': 4.986,
     'tbl_3': 6.957,
     'tbl_4': 8.0,
     'tbl_5': 8.0,
     'tbl_6': 8.0,
     'tbl_7': 6.735,
     'tbl_8': 8.0,
     'tbl_9': 8.0,
     'tbl_10': 8.0,
     'tbl_11': 6.469,
     'tbl_12': 8.0,
     'tbl_13': 8.0,
     'tbl_14': 4.332,
     'tbl_15': 5.595,
     'tbl_16': 8.0,
     'tbl_17': 8.0,
     'tbl_18': 8.0,
     'tbl_19': 5.919,
     'tbl_20': 7.489,
     'tbl_21': 8.0,
     'tbl_22': 8.0,
     'tbl_23': 8.0,
     'tbl_24': 8.0,
     'tbl_25': 7.338,
     'tbl_26': 6.098,
     'tbl_27': 8.0,
     'tbl_28': 8.0,
     'tbl_29': 8.0,
     'tbl_30': 6.345,
     'tbl_31': 6.51,
     'tbl_32': 8.0,
     'tbl_33': 7.057,
     'tbl_34': 8.0,
     'tbl_35': 7.594,
     'tbl_36': 8.0,
     'tbl_37': 6.473,
     'tbl_38': 8.0,
     'L0_rec_W0': 3.251}
    for name, (base, spread) in spreads.items():
        noise = np.random.default_rng([zlib.crc32(name.encode()), seed]).standard_normal(out[name].shape)
        drawn = base * np.exp(spread * noise) if base else spread * noise
        out[name] = jnp.asarray(drawn.astype(out[name].dtype))
    for name, factor in factors.items():
        out[name] = (out[name] * factor).astype(out[name].dtype)
    return out
```

```python
import concourse.bass as bass
from concourse import mybir
from contextlib import ExitStack

FIELDS, D, H = 39, 16, 128
P = 128
TABLES = FIELDS


def build_tower(nc, dense_ctx, ids, tables, W_top1, b_top1, W_top2, b_top2, W_top3, W0, b0, W1, b1, W2, b2, out):
    f32, f32r, i32 = mybir.dt.float32, mybir.dt.float32r, mybir.dt.int32
    ALU = mybir.AluOpType
    ACT = mybir.ActivationFunctionType
    AX = mybir.AxisListType

    BATCH = ids.shape[0]
    CHUNKS = BATCH // P
    COLS = D * P
    HALF = COLS // 2
    SHIFTS = FIELDS // 2 + 1
    PER_TILE = P // FIELDS
    PAIR_TILES = -(-SHIFTS // PER_TILE)
    SHIFTS_OF = [min(PER_TILE, SHIFTS - PER_TILE * t) for t in range(PAIR_TILES)]
    ROWS_OF = [n * FIELDS for n in SHIFTS_OF]
    BANK = 512
    GROUP = BANK // H
    GROUPS = -(-FIELDS // GROUP)
    SLOTS = 4
    SLOT_COUNT = [16 * sum(SHIFTS_OF[s::SLOTS]) for s in range(SLOTS)]
    RING = 4
    SAMPLES_PER_G = P // D
    G_GROUPS = P // SAMPLES_PER_G
    GCOLS = FIELDS + 1
    M1, M2 = W_top1.shape[1], W_top2.shape[1]
    DENSE = dense_ctx.shape[1]

    ACT_GROUPS = (1, 3, 6, 9)
    WIDTH = [min(GROUP, FIELDS - GROUP * g) for g in range(GROUPS)]
    DVE_BEFORE = [sum(WIDTH[h] for h in range(g) if h not in ACT_GROUPS) for g in range(GROUPS + 1)]
    ACT_BEFORE = [sum(WIDTH[h] for h in range(g) if h in ACT_GROUPS) for g in range(GROUPS + 1)]
    DVE_UNITS, ACT_UNITS = DVE_BEFORE[GROUPS], ACT_BEFORE[GROUPS]
    TERMS = ACT_UNITS + 2
    assert TERMS == 17 and P % FIELDS == P - 3 * FIELDS

    XB_SLICE = 2
    L0_FIRST = 2
    G_FIRST = 3
    Z2_SLICES = {11: (0, 20), 12: (20, FIELDS)}
    H1_SLICE, H2_SLICE, Y_SLICE = 13, 14, 15
    MID = 3
    Y_GROUP = 7
    QUARTERS = 4

    ctx = ExitStack()
    with ctx:
        def sb(name, shape, dt=f32):
            return ctx.enter_context(nc.sbuf_tensor(name, shape, dt))

        def sem(name):
            return ctx.enter_context(nc.semaphore(name))

        w1_hi = sb("w1_hi", [P, FIELDS * H], f32r)
        w1_lo = sb("w1_lo", [P, FIELDS * H], f32r)
        w2_t = sb("w2_t", [P, FIELDS * H])
        v_t = sb("v_t", [PER_TILE * FIELDS, PAIR_TILES, H])
        wtop1 = sb("wtop1", [P, 4, M1])
        wtop2 = sb("wtop2", [P, M1 // P, M2])
        wtop3 = sb("wtop3", [P, M2 // P])
        btop1 = sb("btop1", [P, M1 // P])
        btop2 = sb("btop2", [P, M2 // P])
        b0_col = sb("b0_col", [P, 1])
        b2_col = sb("b2_col", [P, 1])
        b0_sum = sb("b0_sum", [P, 1])
        b2_sum = sb("b2_sum", [P, 1])
        b1_rows = sb("b1_rows", [P, H])
        ident = sb("ident", [P, P])
        own = sb("own", [P, SAMPLES_PER_G])
        dense_t = sb("dense_t", [DENSE, BATCH])
        ids_sb = sb("ids_sb", [P, CHUNKS, FIELDS], i32)
        idx = sb("idx", [P, FIELDS], i32)
        e_in = sb("e_in", [P, FIELDS, D])
        e_mid = sb("e_mid", [P, 2 * FIELDS, D])
        e_cur = sb("e_cur", [P, FIELDS, D])
        x0_t = sb("x0_t", [2 * FIELDS, COLS])
        x0_rep = sb("x0_rep", [PER_TILE * FIELDS, HALF])
        pairs = sb("pairs", [PER_TILE * FIELDS, SLOTS, HALF])
        x1_hi = sb("x1_hi", [P, COLS], f32r)
        x1_lo = sb("x1_lo", [P, COLS], f32r)
        terms = sb("terms", [P, 2, TERMS, H])
        x2_s = sb("x2_s", [P, D, H])
        x2_r = sb("x2_r", [P, G_GROUPS, H])
        xb = [sb(f"xb{i}", [P, G_GROUPS, FIELDS]) for i in range(3)]
        blocks = sb("blocks", [P, 2, SAMPLES_PER_G, GCOLS])
        g_t = sb("g_t", [P, GCOLS, P])
        z0_part = sb("z0_part", [P, P])
        z0_new = sb("z0_new", [P, P])
        z0_old = sb("z0_old", [P, P])
        z2_sb = sb("z2_sb", [P, P])
        h1_sb = sb("h1_sb", [P, M1 // P, P])
        h2_sb = sb("h2_sb", [P, M2 // P, P])
        y_sb = sb("y_sb", [1, P])
        w12_raw = g_t[:, :, :].rearrange("p j b -> p (j b)")[:, 0:FIELDS * H]
        w0_raw = x2_s[:, :, :].rearrange("p d h -> p (d h)")[:, 0:FIELDS * FIELDS]
        v_raw = x2_r[:, :, :].rearrange("p g h -> p (g h)")[:, 0:SHIFTS * FIELDS]
        dense_raw = terms[:, 0, 0, :].rearrange("p (c e) -> p c e", e=DENSE)

        ring = ctx.enter_context(nc.psum_tensor("ring", [P, RING, BANK], f32))
        l0_ps = ctx.enter_context(nc.psum_tensor("l0_ps", [P, HALF], f32))
        side = ctx.enter_context(nc.psum_tensor("side", [P, 2, BANK], f32))

        y_dram = out.rearrange("b o -> o b")
        x2_dram = nc.dram_tensor("x2_scratch", [D, P, H], f32, kind="Internal").ap()

        w0_in, w1_in, w2_in, ids_in, dense_in, small_in, top_in = (
            sem(n) for n in ("w0_in", "w1_in", "w2_in", "ids_in", "dense_in", "small_in", "top_in"))
        consts_made, zeroed, own_made = sem("consts_made"), sem("zeroed"), sem("own_made")
        bias_sums, v_made = sem("bias_sums"), sem("v_made")
        setup_ps, setup_hi, setup_lo = sem("setup_ps"), sem("setup_hi"), sem("setup_lo")
        idx_ready, gathered, e_cur_ready, e_mid_ready, xb_moved, xb_kept = (
            sem("idx_ready"), sem("gathered"), sem("e_cur_ready"), sem("e_mid_ready"), sem("xb_moved"),
            sem("xb_kept"))
        x0t_ps, x0t_ready, xb_ps, xb_ready = sem("x0t_ps"), sem("x0t_ready"), sem("xb_ps"), sem("xb_ready")
        rep_in = sem("rep_in")
        pair_in = [sem(f"pair_in{s}") for s in range(SLOTS)]
        pair_made, pair_used = sem("pair_made"), sem("pair_used")
        x1_hi_ready, x1_lo_ready, z0_summed, z0_ready, z0_kept = (
            sem("x1_hi_ready"), sem("x1_lo_ready"), sem("z0_summed"), sem("z0_ready"), sem("z0_kept"))
        y_group, act_group, dve_unit = sem("y_group"), sem("act_group"), sem("dve_unit")
        folded, x2_done = sem("folded"), sem("x2_done")
        x2_out, x2_in = sem("x2_out"), sem("x2_in")
        block_made, g_ps, g_ready = sem("block_made"), sem("g_ps"), sem("g_ready")
        z2_ps, z2_ready, h1_ps, h1_ready, h2_ps, h2_ready, y_ps, y_ready, y_out = (
            sem(n) for n in ("z2_ps", "z2_ready", "h1_ps", "h1_ready", "h2_ps", "h2_ready", "y_ps", "y_ready",
                             "y_out"))

        block = ctx.enter_context(nc.Block())

        def after(eng, semaphore, count):
            if not isinstance(count, int) or count > 0:
                eng.wait_ge(semaphore, count)

        def steps(eng, step):
            step(-1, first=True, layer1=False, following=True, previous=False, gathers=True)
            step(0, layer1=True, following=True, previous=False, gathers=True)
            with eng.Fori(1, CHUNKS - 2) as c:
                step(c, layer1=True, following=True, previous=True, gathers=True)
            step(CHUNKS - 2, layer1=True, following=True, previous=True, gathers=False)
            step(CHUNKS - 1, layer1=True, following=False, previous=True, gathers=False)
            step(CHUNKS, layer1=False, following=False, previous=True, gathers=False)

        SETUP_W1, SETUP_W2 = GROUPS, GROUPS
        SETUP_V = -(-PAIR_TILES // 4)
        SETUP_DENSE = CHUNKS // 4
        SETUP = SETUP_V + SETUP_DENSE + SETUP_W1 + SETUP_W2

        @block.sync
        def _(sp):
            sp.dma_start(ids_sb[:, :, :], ids.rearrange("(c p) f -> p c f", p=P)).then_inc(ids_in, 16)
            sp.dma_start(w0_raw, W0).then_inc(w0_in, 16)
            sp.dma_start(dense_raw, dense_ctx.rearrange("(c p) e -> p c e", p=P)).then_inc(dense_in, 16)
            sp.dma_start(w12_raw, W1).then_inc(w1_in, 16)
            col = lambda a: a.rearrange("(p o) -> p o", o=1)
            sp.dma_start(b0_col[:, :], col(b0)).then_inc(small_in, 16)
            sp.dma_start(b2_col[:, :], col(b2)).then_inc(small_in, 16)
            sp.dma_start(b1_rows[:, :], b1.rearrange("(o h) -> o h", o=1).to_broadcast([P, H])).then_inc(small_in, 16)
            sp.dma_start(wtop1[:, 0:3, :], W_top1[0:3 * P, :].rearrange("(t p) m -> p t m", p=P)).then_inc(top_in, 16)
            sp.dma_start(wtop1[0:DENSE, 3, :], W_top1[3 * P:, :]).then_inc(top_in, 16)
            sp.dma_start(wtop2[:, :, :], W_top2.rearrange("(t p) m -> p t m", p=P)).then_inc(top_in, 16)
            with nc.allow_non_contiguous_dma(reason="a few hundred words onto the partitions"):
                sp.dma_start(wtop3[:, :], W_top3.rearrange("(t p) o -> p (t o)", p=P)).then_inc(top_in, 16)
                sp.dma_start(btop1[:, :], b_top1.rearrange("(t p) -> p t", p=P)).then_inc(top_in, 16)
                sp.dma_start(btop2[:, :], b_top2.rearrange("(t p) -> p t", p=P)).then_inc(top_in, 16)
            sp.wait_ge(setup_ps, SETUP - SETUP_W2)
            sp.dma_start(w12_raw, W2).then_inc(w2_in, 16)

            def step(c, layer1, following, previous, gathers, first=False):
                def pair_tile(half, t):
                    before = t - SLOTS if t >= SLOTS else (t + SLOTS if t + SLOTS < PAIR_TILES else t) - PAIR_TILES
                    after(sp, pair_used, PAIR_TILES * (2 * (c + 1) + half) + before + 1)
                    for n in range(SHIFTS_OF[t]):
                        s = PER_TILE * t + n
                        sp.dma_start(pairs[n * FIELDS:(n + 1) * FIELDS, t % SLOTS, :],
                                     x0_t[s:s + FIELDS, half * HALF:(half + 1) * HALF]
                                     ).then_inc(pair_in[t % SLOTS], 16)

                def rep(half):
                    after(sp, x0t_ready, 4 * (c + 1) + 2 * half + 2)
                    after(sp, pair_made, PAIR_TILES * (2 * (c + 1) + half))
                    for n in range(PER_TILE):
                        sp.dma_start(x0_rep[n * FIELDS:(n + 1) * FIELDS, :],
                                     x0_t[0:FIELDS, half * HALF:(half + 1) * HALF]).then_inc(rep_in, 16)

                def x2_write(chunk, q):
                    n = D // QUARTERS
                    after(sp, x2_done, D * chunk + n * (q + 1))
                    after(sp, x2_in, 16 * chunk)
                    sp.dma_start(x2_dram[n * q:n * (q + 1), :, :].rearrange("d b h -> b d h"),
                                 x2_s[:, n * q:n * (q + 1), :]).then_inc(x2_out, 16)

                if previous:
                    x2_write(c - 1, QUARTERS - 1)
                    after(sp, x2_out, 16 * QUARTERS * c)
                    after(sp, g_ps, G_GROUPS * (c - 1))
                    sp.dma_start(x2_r[:, :, :],
                                 x2_dram.rearrange("d (b g) h -> (d b) g h", g=G_GROUPS)
                                 ).then_inc(x2_in, 16)
                for half in range(2):
                    if following:
                        rep(half)
                    for t in range(PAIR_TILES):
                        if following:
                            pair_tile(half, t)
                        if layer1 and t == PAIR_TILES // 2 and half == 1:
                            x2_write(c, 1)
                    if layer1:
                        x2_write(c, 2 * half)
                if previous:
                    after(sp, y_ready, c)
                    sp.dma_start(y_dram[:, bass.ds((c - 1) * P, P)], y_sb[0:1, :]).then_inc(y_out, 16)

            steps(sp, step)
            sp.wait_ge(y_out, 16 * CHUNKS)
            sp.wait_ge(x2_out, 16 * QUARTERS * CHUNKS)

        @block.gpsimd
        def _(pool):
            def gather(chunk, f):
                nc.gpsimd.indirect_dma_start(
                    e_in[:, f, :], None, tables[f], bass.IndirectOffsetOnAxis(ap=idx[:, f:f + 1], axis=0)
                ).then_inc(gathered, 16)

            pool.wait_ge(ids_in, 16)
            nc.gpsimd.tensor_copy(idx[:, :], ids_sb[:, 0, :]).then_inc(idx_ready, 1)
            nc.gpsimd.memset(ident[:, :], 0.0).then_inc(zeroed, 1)
            pool.wait_ge(zeroed, 1)
            nc.gpsimd.affine_select(out=ident[:, :], in_=ident[:, :], compare_op=ALU.not_equal, fill=1.0, base=0,
                                    pattern=[[-1, P]], channel_multiplier=1).then_inc(consts_made, 1)
            pool.wait_ge(idx_ready, 1)
            for f in range(FIELDS):
                gather(0, f)

            def step(c, layer1, following, previous, gathers, first=False):
                def next_index():
                    pool.wait_ge(gathered, 16 * FIELDS * (c + 2))
                    nc.gpsimd.tensor_copy(idx[:, :], ids_sb[:, c + 2, :]).then_inc(idx_ready, 1)

                if not layer1:
                    if gathers:
                        next_index()
                        pool.wait_ge(idx_ready, c + 3)
                        pool.wait_ge(e_mid_ready, c + 2)
                        for f in range(FIELDS):
                            gather(c + 2, f)
                    return
                for d in range(D):
                    t = terms[:, d % 2]
                    n = D * c + d
                    after(pool, act_group, len(ACT_GROUPS) * (n + 1))
                    after(pool, dve_unit, DVE_UNITS * (n + 1))
                    if d == 0:
                        after(pool, x2_out, 16 * QUARTERS * c)
                    for i, w in enumerate((8, 4, 2, 1)):
                        nc.gpsimd.tensor_tensor(t[:, 0:w, :], t[:, 0:w, :], t[:, w:2 * w, :],
                                                ALU.add).then_inc(folded, 1)
                        if i == 0 and d == 0 and gathers:
                            next_index()
                            pool.wait_ge(idx_ready, c + 3)
                            pool.wait_ge(e_mid_ready, c + 2)
                        pool.wait_ge(folded, 4 * n + i + 1)
                    nc.gpsimd.tensor_tensor(x2_s[:, d, :], t[:, 0, :], t[:, TERMS - 1, :],
                                            ALU.add).then_inc(x2_done, 1)
                    if gathers:
                        for f in range(3 * d, min(3 * d + 3, FIELDS)):
                            gather(c + 2, f)

            steps(pool, step)

        @block.scalar
        def _(act):
            def setup_copy(batch, dst, rows, width):
                act.wait_ge(setup_ps, batch + 1)
                nc.scalar.activation(dst, ring[0:rows, batch % RING, 0:width], ACT.Copy).then_inc(setup_hi, 1)

            batch = 0
            for q in range(SETUP_V):
                act.wait_ge(setup_ps, batch + 1)
                for i, t in enumerate(range(4 * q, min(4 * q + 4, PAIR_TILES))):
                    rows = ROWS_OF[t]
                    last = nc.scalar.activation(v_t[0:rows, t, :], ring[0:rows, batch % RING, i * H:(i + 1) * H],
                                                ACT.Copy)
                last.then_inc(setup_hi, 1)
                batch += 1
            for q in range(SETUP_DENSE):
                setup_copy(batch, dense_t[:, BANK * q:BANK * (q + 1)], DENSE, BANK)
                batch += 1
            for dst in (w1_hi, w2_t):
                for q in range(GROUPS):
                    n = min(BANK, FIELDS * H - BANK * q)
                    setup_copy(batch, dst[:, BANK * q:BANK * q + n], P, n)
                    batch += 1

            def step(c, layer1, following, previous, gathers, first=False):
                def x1_half(chunk, half):
                    after(act, pair_used, 14 * chunk + 7 * half + 7)
                    after(act, y_group, GROUPS * (D * (chunk - 1) + D // 2 * (half + 1)))
                    nc.scalar.activation(x1_hi[:, half * HALF:(half + 1) * HALF], l0_ps[:, :], ACT.Identity,
                                         bias=b0_col[:, 0:1]).then_inc(x1_hi_ready, 1)

                def side_work(d):
                    e = d - 1
                    if following and 0 <= e < 2:
                        for q in (2 * e, 2 * e + 1):
                            after(act, x0t_ps, 4 * (c + 1) + q + 1)
                            for s in range(SLOTS):
                                after(act, pair_in[s], SLOT_COUNT[s] * 2 * (c + 1))
                            after(act, rep_in, 16 * PER_TILE * 2 * (c + 1))
                            after(act, xb_ps, 2 * (c + 1))
                            nc.scalar.activation(x0_t[:, q * BANK:(q + 1) * BANK], side[0:2 * FIELDS, q % 2, :],
                                                 ACT.Copy).then_inc(x0t_ready, 1)
                    if following and e == XB_SLICE:
                        n = G_GROUPS // 2
                        for q in range(2):
                            after(act, xb_ps, 2 * (c + 1) + q + 1)
                            after(act, xb_kept, c + 1)
                            nc.scalar.activation(xb[0][:, n * q:n * (q + 1), :], side[:, q, 0:n * FIELDS],
                                                 ACT.Copy).then_inc(xb_ready, 1)
                    if following and e == L0_FIRST + PAIR_TILES - 1:
                        x1_half(c + 1, 0)
                    if previous and G_FIRST <= e < G_FIRST + G_GROUPS // 2:
                        for g in (2 * (e - G_FIRST), 2 * (e - G_FIRST) + 1):
                            n = G_GROUPS * (c - 1) + g
                            after(act, g_ps, n + 1)
                            after(act, h1_ps, c - 1)
                            nc.scalar.activation(
                                g_t[:, :, g::G_GROUPS],
                                side[:, g % 2, 0:SAMPLES_PER_G * GCOLS].rearrange("p (b j) -> p j b", j=GCOLS),
                                ACT.Copy).then_inc(g_ready, 1)
                    if previous and e == 12:
                        after(act, z2_ps, c)
                        after(act, h1_ps, c - 1)
                        nc.scalar.activation(z2_sb[:, :], side[:, 0, 0:P], ACT.Identity,
                                             bias=b2_sum[:, 0:1]).then_inc(z2_ready, 1)
                    if previous and e == H1_SLICE:
                        after(act, h1_ps, c)
                        after(act, h2_ps, c - 1)
                        for m in range(M1 // P):
                            last = nc.scalar.activation(h1_sb[:, m, :], side[:, 1, m * P:(m + 1) * P], ACT.Relu,
                                                        bias=btop1[:, m:m + 1])
                        last.then_inc(h1_ready, 1)
                    if previous and e == H2_SLICE:
                        after(act, h2_ps, c)
                        after(act, y_ps, c - 1)
                        for m in range(M2 // P):
                            last = nc.scalar.activation(h2_sb[:, m, :], side[:, 0, m * P:(m + 1) * P], ACT.Relu,
                                                        bias=btop2[:, m:m + 1])
                        last.then_inc(h2_ready, 1)

                if not first:
                    if layer1:
                        x1_half(c, 1)
                for d in range(D):
                    if not layer1:
                        side_work(d)
                        continue
                    n = D * c + d
                    if d == 0:
                        act.wait_ge(e_cur_ready, c + 1)
                    after(act, x2_done, n - 1)
                    for g in range(GROUPS):
                        if g == MID:
                            side_work(d)
                        if g not in ACT_GROUPS:
                            continue
                        after(act, y_group, GROUPS * n + g + 1)
                        for i in range(WIDTH[g]):
                            j = GROUP * g + i
                            last = nc.scalar.activation(terms[:, d % 2, ACT_BEFORE[g] + i, :],
                                                        ring[:, (GROUPS * d + g) % RING, i * H:(i + 1) * H], ACT.Copy,
                                                        scale=e_cur[:, j, d:d + 1])
                        last.then_inc(act_group, 1)
                if previous:
                    if not layer1:
                        side_work(D)
                    after(act, y_ps, c)
                    after(act, y_out, 16 * (c - 1))
                    nc.scalar.activation(y_sb[0:1, :], side[0:1, 1, 0:P], ACT.Copy).then_inc(y_ready, 1)

            act.wait_ge(small_in, 48)
            act.wait_ge(bias_sums, 2)
            act.wait_ge(top_in, 96)
            steps(act, step)

        @block.vector
        def _(dve):
            dve.wait_ge(w0_in, 16)
            nc.vector.tensor_copy(v_raw[:, 0:FIELDS], w0_raw[:, 0:FIELDS * FIELDS:FIELDS + 1])
            for s in range(1, SHIFTS):
                for i0, i1, a, b in ((0, FIELDS - s, s, FIELDS * s),
                                     (FIELDS - s, FIELDS, s - FIELDS, FIELDS * (s - FIELDS))):
                    step40 = FIELDS + 1
                    n = i1 - i0
                    x = step40 * i0 + a
                    y = step40 * i0 + b
                    last = nc.vector.tensor_tensor(
                        v_raw[:, s * FIELDS + i0:s * FIELDS + i1],
                        w0_raw[:, x:x + step40 * (n - 1) + 1:step40],
                        w0_raw[:, y:y + step40 * (n - 1) + 1:step40], ALU.add)
            last.then_inc(v_made, 1)
            dve.wait_ge(small_in, 48)
            nc.vector.tensor_scalar(b0_sum[:, :], b0_col[:, :], float(D), None, ALU.mult).then_inc(bias_sums, 1)
            nc.vector.tensor_scalar(b2_sum[:, :], b2_col[:, :], float(D), None, ALU.mult).then_inc(bias_sums, 1)
            dve.wait_ge(consts_made, 1)
            nc.vector.tensor_reduce(own[:, :], ident[:, :].rearrange("p (d b) -> p b d", d=D), AX.X,
                                    ALU.add).then_inc(own_made, 1)
            dve.wait_ge(own_made, 1)
            for i in range(2):
                nc.vector.tensor_copy(blocks[:, i, :, FIELDS], own[:, :])
            for q in range(GROUPS):
                batch = SETUP_V + SETUP_DENSE + q
                n = min(BANK, FIELDS * H - BANK * q)
                dve.wait_ge(setup_hi, batch + 1)
                nc.vector.tensor_tensor(w1_lo[:, BANK * q:BANK * q + n], ring[:, batch % RING, 0:n],
                                        w1_hi[:, BANK * q:BANK * q + n].bitcast(f32),
                                        ALU.subtract).then_inc(setup_lo, 1)

            def step(c, layer1, following, previous, gathers, first=False):
                def x1_half(chunk, half):
                    x = slice(half * HALF, (half + 1) * HALF)
                    after(dve, x1_hi_ready, 2 * chunk + half + 1)
                    nc.vector.scalar_tensor_tensor(out=x1_lo[:, x], in0=l0_ps[:, :], scalar=b0_col[:, 0:1],
                                                   in1=x1_hi[:, x].bitcast(f32), op0=ALU.add,
                                                   op1=ALU.subtract).then_inc(x1_lo_ready, 1)
                    dst = z0_part if half == 0 else z0_new
                    if half == 1 and not (isinstance(chunk, int) and chunk == 0):
                        after(dve, h1_ps, chunk - 1)
                        nc.vector.tensor_copy(z0_old[:, :], z0_new[:, :]).then_inc(z0_kept, 1)
                        dve.wait_ge(z0_kept, chunk)
                    nc.vector.tensor_reduce(dst[:, :], l0_ps[:, :].rearrange("p (d b) -> p b d", b=P),
                                            AX.X, ALU.add).then_inc(z0_summed, 1)
                    if half == 1:
                        after(dve, z0_summed, 2 * chunk + 2)
                        nc.vector.scalar_tensor_tensor(out=z0_new[:, :], in0=z0_part[:, :], scalar=b0_sum[:, 0:1],
                                                       in1=z0_new[:, :], op0=ALU.add,
                                                       op1=ALU.add).then_inc(z0_ready, 1)

                def side_work(d):
                    if following and d == 0:
                        after(dve, gathered, 16 * FIELDS * (c + 2))
                        after(dve, x0t_ps, 4 * (c + 1))
                        after(dve, e_cur_ready, c + 1)
                        for i in range(2):
                            last = nc.vector.tensor_copy(e_mid[:, i * FIELDS:(i + 1) * FIELDS, :], e_in[:, :, :])
                        last.then_inc(e_mid_ready, 1)
                    if d == 1 and not first and not (isinstance(c, int) and c < 0):
                        if previous:
                            after(dve, xb_kept, c)
                            nc.vector.tensor_copy(xb[2][:, :, :], xb[1][:, :, :]).then_inc(xb_moved, 1)
                        if layer1:
                            after(dve, xb_ready, 2 * (c + 1))
                            after(dve, xb_moved, c)
                            nc.vector.tensor_copy(xb[1][:, :, :], xb[0][:, :, :]).then_inc(xb_kept, 1)
                    if following and d >= L0_FIRST:
                        half, t = divmod(d - L0_FIRST, PAIR_TILES)
                        rows = ROWS_OF[t]
                        s = t % SLOTS
                        k = 2 * (c + 1) + half
                        after(dve, rep_in, 16 * PER_TILE * (k + 1))
                        after(dve, pair_in[s], SLOT_COUNT[s] * k + 16 * sum(SHIFTS_OF[s:t + 1:SLOTS]))
                        nc.vector.tensor_tensor(pairs[0:rows, s, :], x0_rep[0:rows, :], pairs[0:rows, s, :],
                                                ALU.mult).then_inc(pair_made, 1)
                    if following and d == L0_FIRST + PAIR_TILES:
                        x1_half(c + 1, 0)
                    if previous and G_FIRST <= d < G_FIRST + G_GROUPS // 2:
                        if d == G_FIRST:
                            after(dve, xb_moved, c)
                        for g in (2 * (d - G_FIRST), 2 * (d - G_FIRST) + 1):
                            n = G_GROUPS * (c - 1) + g
                            after(dve, g_ps, n - g if g < 2 else n - 1)
                            shape = [P, SAMPLES_PER_G, FIELDS]
                            nc.vector.tensor_tensor(
                                blocks[:, g % 2, :, 0:FIELDS],
                                xb[2][:, g:g + 1, :].to_broadcast(shape),
                                own[:, :].unsqueeze(2).to_broadcast(shape), ALU.mult).then_inc(block_made, 1)

                if layer1:
                    after(dve, act_group, len(ACT_GROUPS) * D * c)
                    after(dve, dve_unit, DVE_UNITS * D * c)
                    after(dve, e_mid_ready, c + 1)
                    nc.vector.tensor_copy(e_cur[:, :, :], e_mid[:, 0:FIELDS, :]).then_inc(e_cur_ready, 1)
                    x1_half(c, 1)
                    dve.wait_ge(e_cur_ready, c + 1)
                for d in range(D):
                    if not layer1:
                        side_work(d)
                        continue
                    n = D * c + d
                    after(dve, x2_done, n - 1)
                    unit = 0
                    for g in range(GROUPS):
                        if g == MID:
                            side_work(d)
                        if g in ACT_GROUPS:
                            continue
                        after(dve, y_group, GROUPS * n + g + 1)
                        for i in range(WIDTH[g]):
                            j = GROUP * g + i
                            y = ring[:, (GROUPS * d + g) % RING, i * H:(i + 1) * H]
                            acc = terms[:, d % 2, ACT_UNITS + unit % 2, :]
                            if unit == 0:
                                nc.vector.scalar_tensor_tensor(out=acc, in0=y, scalar=e_cur[:, j, d:d + 1],
                                                               in1=b1_rows[:, :], op0=ALU.mult,
                                                               op1=ALU.add).then_inc(dve_unit, 1)
                            elif unit == 1:
                                nc.vector.tensor_scalar(acc, y, e_cur[:, j, d:d + 1], None,
                                                        ALU.mult).then_inc(dve_unit, 1)
                            else:
                                after(dve, dve_unit, DVE_UNITS * n + unit - 1)
                                nc.vector.scalar_tensor_tensor(out=acc, in0=y, scalar=e_cur[:, j, d:d + 1],
                                                               in1=acc, op0=ALU.mult,
                                                               op1=ALU.add).then_inc(dve_unit, 1)
                            unit += 1

            steps(dve, step)

        @block.tensor
        def _(pe):
            pe.wait_ge(consts_made, 1)
            batch = 0

            def bank_free(batch):
                after(pe, setup_hi, batch - RING + 1)
                after(pe, setup_lo, min(batch - RING + 1 - SETUP_V - SETUP_DENSE, SETUP_W1))

            pe.wait_ge(v_made, 1)
            for q in range(SETUP_V):
                bank_free(batch)
                for i, t in enumerate(range(4 * q, min(4 * q + 4, PAIR_TILES))):
                    x = PER_TILE * FIELDS * t
                    rows = ROWS_OF[t]
                    last = nc.tensor.transpose(ring[0:rows, batch % RING, i * H:(i + 1) * H], v_raw[:, x:x + rows],
                                               ident[:, :])
                last.then_inc(setup_ps, 1)
                batch += 1
            pe.wait_ge(dense_in, 16)
            for q in range(SETUP_DENSE):
                bank_free(batch)
                for i in range(4):
                    last = nc.tensor.transpose(ring[0:DENSE, batch % RING, i * P:(i + 1) * P],
                                               dense_raw[:, 4 * q + i, :], ident[:, :])
                last.then_inc(setup_ps, 1)
                batch += 1
            for loaded in (w1_in, w2_in):
                pe.wait_ge(loaded, 16)
                for q in range(GROUPS):
                    bank_free(batch)
                    for i, j in enumerate(range(GROUP * q, min(GROUP * (q + 1), FIELDS))):
                        last = nc.tensor.transpose(ring[:, batch % RING, i * H:(i + 1) * H],
                                                   w12_raw[:, j * H:(j + 1) * H], ident[:, :])
                    last.then_inc(setup_ps, 1)
                    batch += 1

            def step(c, layer1, following, previous, gathers, first=False):
                def layer0(d):
                    half, t = divmod(d - L0_FIRST, PAIR_TILES)
                    rows = ROWS_OF[t]
                    n = 2 * (c + 1) + half
                    if t == 0:
                        after(pe, x1_hi_ready, n)
                        after(pe, x1_lo_ready, n)
                        after(pe, z0_summed, n)
                    after(pe, pair_made, PAIR_TILES * n + t + 1)
                    for x in range(0, HALF, BANK):
                        last = nc.tensor.matmul(l0_ps[:, x:x + BANK], v_t[0:rows, t, :], pairs[0:rows, t % SLOTS, x:x + BANK],
                                                start=(t == 0), stop=(t == PAIR_TILES - 1))
                    last.then_inc(pair_used, 1)

                def layer_y():
                    after(pe, h2_ready, c)
                    for k in range(M2 // P):
                        last = nc.tensor.matmul(side[0:1, 1, 0:P], wtop3[:, k:k + 1], h2_sb[:, k, :],
                                                start=(k == 0), stop=(k == M2 // P - 1))
                    last.then_inc(y_ps, 1)

                def end_of_slice(d):
                    if following and d < 2:
                        if d == 0:
                            after(pe, e_mid_ready, c + 2)
                            after(pe, h2_ready, c - 1)
                            after(pe, y_ready, c - 1)
                        for q in (2 * d, 2 * d + 1):
                            after(pe, x0t_ready, 4 * (c + 1) + q - 1)
                            for i in range(4):
                                last = nc.tensor.transpose(side[0:2 * FIELDS, q % 2, i * P:(i + 1) * P],
                                                           e_mid[:, :, 4 * q + i], ident[:, :])
                            last.then_inc(x0t_ps, 1)
                    if following and d == XB_SLICE:
                        n = G_GROUPS // 2
                        if not layer1:
                            after(pe, x0t_ready, 4 * (c + 1) + 4)
                        for q in range(2):
                            for i in range(n):
                                r = q * n + i
                                last = nc.tensor.transpose(side[:, q, i * FIELDS:(i + 1) * FIELDS],
                                                           x0_t[0:FIELDS, r::G_GROUPS],
                                                           ident[0:FIELDS, 0:FIELDS])
                            last.then_inc(xb_ps, 1)
                    if previous and G_FIRST <= d < G_FIRST + G_GROUPS // 2:
                        if d == G_FIRST:
                            after(pe, x2_in, 16 * c)
                            if not (isinstance(c, int) and c >= CHUNKS - 1):
                                after(pe, xb_ready, 2 * (c + 2))
                            after(pe, h2_ready, c - 1)
                            after(pe, y_ready, c - 1)
                        for g in (2 * (d - G_FIRST), 2 * (d - G_FIRST) + 1):
                            n = G_GROUPS * (c - 1) + g
                            after(pe, block_made, n + 1)
                            if g >= 2:
                                after(pe, g_ready, n - 1)
                            nc.tensor.matmul(side[:, g % 2, 0:SAMPLES_PER_G * GCOLS], x2_r[:, g, :],
                                             blocks[:, g % 2, :, :].rearrange("p b j -> p (b j)"),
                                             start=True, stop=True).then_inc(g_ps, 1)
                    if previous and d in Z2_SLICES:
                        j0, j1 = Z2_SLICES[d]
                        after(pe, g_ready, G_GROUPS * c)
                        for j in range(j0, j1):
                            last = nc.tensor.matmul(side[:, 0, 0:P], w2_t[:, j * H:(j + 1) * H], g_t[:, j, :],
                                                    start=(j == 0), stop=(j == FIELDS - 1))
                        if j1 == FIELDS:
                            last.then_inc(z2_ps, 1)
                    if previous and d == H1_SLICE:
                        after(pe, z2_ready, c)
                        after(pe, z0_ready, c)
                        if layer1:
                            after(pe, z0_kept, c)
                        z0 = z0_old if layer1 else z0_new
                        for m in range(M1 // P):
                            for k, z in enumerate((z0[:, :], g_t[:, FIELDS, :], z2_sb[:, :],
                                                   dense_t[:, bass.ds((c - 1) * P, P)])):
                                rows = DENSE if k == 3 else P
                                last = nc.tensor.matmul(side[:, 1, m * P:(m + 1) * P],
                                                        wtop1[0:rows, k, m * P:(m + 1) * P], z,
                                                        start=(k == 0), stop=(k == 3))
                        last.then_inc(h1_ps, 1)
                    if previous and d == H2_SLICE:
                        after(pe, h1_ready, c)
                        for m in range(M2 // P):
                            for k in range(M1 // P):
                                last = nc.tensor.matmul(side[:, 0, m * P:(m + 1) * P],
                                                        wtop2[:, k, m * P:(m + 1) * P], h1_sb[:, k, :],
                                                        start=(k == 0), stop=(k == M1 // P - 1))
                        last.then_inc(h2_ps, 1)
                    if previous and not layer1 and d == Y_SLICE:
                        layer_y()
                    if following and d >= L0_FIRST:
                        layer0(d)

                for d in range(D):
                    if layer1:
                        if d % (D // 2) == 0:
                            k = 2 * c + d // (D // 2) + 1
                            after(pe, x1_hi_ready, k)
                            after(pe, x1_lo_ready, k)
                        x = slice(d * P, (d + 1) * P)
                        for g in range(GROUPS):
                            if previous and d == Y_SLICE and g == Y_GROUP:
                                layer_y()
                            width = WIDTH[g] * H
                            w = slice(g * BANK, g * BANK + width)
                            if following and d == XB_SLICE and g == GROUPS - 1:
                                after(pe, x0t_ready, 4 * (c + 1) + 4)
                            slice_before, b = (D * c + d, g - RING) if g >= RING else (D * c + d - 1, g - RING + GROUPS)
                            if b in ACT_GROUPS:
                                after(pe, act_group, len(ACT_GROUPS) * slice_before
                                      + sum(h <= b for h in ACT_GROUPS))
                            else:
                                after(pe, dve_unit, DVE_UNITS * slice_before + DVE_BEFORE[b + 1])
                            acc = ring[:, (GROUPS * d + g) % RING, 0:width]
                            nc.tensor.matmul(acc, x1_hi[:, x], w1_hi[:, w], start=True, stop=False)
                            nc.tensor.matmul(acc, x1_hi[:, x], w1_lo[:, w], start=False, stop=False)
                            nc.tensor.matmul(acc, x1_lo[:, x], w1_hi[:, w], start=False,
                                             stop=True).then_inc(y_group, 1)
                    end_of_slice(d)

            pe.wait_ge(top_in, 96)
            pe.wait_ge(setup_hi, SETUP)
            pe.wait_ge(setup_lo, SETUP_W1)
            steps(pe, step)


_TABLES = [f"tbl_{f}" for f in range(TABLES)]
_INS = (["dense_ctx", "ids"] + _TABLES + ["W_top1", "b_top1", "W_top2", "b_top2", "W_top3"]
        + [f"L0_rec_{kind}{layer}" for layer in range(3) for kind in "Wb"])


def kernel(**inputs):
    import numpy as _np
    import concourse.bacc as _bacc
    from concourse import mybir as _mybir
    from concourse.bass_utils import run_bass_kernel_spmd as _run

    nc = _bacc.Bacc("TRN2", target_bir_lowering=False, num_devices=1)
    arrays, aps = {}, {}
    for name in _INS:
        a = _np.ascontiguousarray(inputs[name])
        arrays[f"in_{name}"] = a
        aps[name] = nc.dram_tensor(f"in_{name}", a.shape, _mybir.dt.from_np(a.dtype), kind="ExternalInput").ap()
    batch = arrays["in_ids"].shape[0]
    out = nc.dram_tensor("out_y", (batch, 1), _mybir.dt.float32, kind="ExternalOutput").ap()
    build_tower(nc, aps["dense_ctx"], aps["ids"], [aps[t] for t in _TABLES], aps["W_top1"], aps["b_top1"],
                aps["W_top2"], aps["b_top2"], aps["W_top3"], aps["L0_rec_W0"], aps["L0_rec_b0"], aps["L0_rec_W1"],
                aps["L0_rec_b1"], aps["L0_rec_W2"], aps["L0_rec_b2"], out)
    return _run(nc, [arrays], core_ids=[0]).results[0]["out_y"]
```

```python
import concourse.bass as bass
from concourse import mybir
from contextlib import ExitStack

FIELDS, D, H = 39, 16, 128
P = 128
TABLES = FIELDS


def build_tower(nc, dense_ctx, ids, tables, W_top1, b_top1, W_top2, b_top2, W_top3, W0, b0, W1, b1, W2, b2, out):
    f32, f32r, i32 = mybir.dt.float32, mybir.dt.float32r, mybir.dt.int32
    ALU = mybir.AluOpType
    ACT = mybir.ActivationFunctionType
    AX = mybir.AxisListType

    BATCH = ids.shape[0]
    CHUNKS = BATCH // P
    COLS = D * P
    HALF = COLS // 2
    SHIFTS = FIELDS // 2 + 1
    PER_TILE = P // FIELDS
    PAIR_TILES = -(-SHIFTS // PER_TILE)
    SHIFTS_OF = [min(PER_TILE, SHIFTS - PER_TILE * t) for t in range(PAIR_TILES)]
    ROWS_OF = [n * FIELDS for n in SHIFTS_OF]
    BANK = 512
    GROUP = BANK // H
    GROUPS = -(-FIELDS // GROUP)
    SLOTS = 4
    SLOT_COUNT = [16 * sum(SHIFTS_OF[s::SLOTS]) for s in range(SLOTS)]
    RING = 4
    SAMPLES_PER_G = P // D
    G_GROUPS = P // SAMPLES_PER_G
    GCOLS = FIELDS + 1
    M1, M2 = W_top1.shape[1], W_top2.shape[1]
    DENSE = dense_ctx.shape[1]

    ACT_GROUPS = (1, 3, 6, 9)
    WIDTH = [min(GROUP, FIELDS - GROUP * g) for g in range(GROUPS)]
    DVE_BEFORE = [sum(WIDTH[h] for h in range(g) if h not in ACT_GROUPS) for g in range(GROUPS + 1)]
    ACT_BEFORE = [sum(WIDTH[h] for h in range(g) if h in ACT_GROUPS) for g in range(GROUPS + 1)]
    DVE_UNITS, ACT_UNITS = DVE_BEFORE[GROUPS], ACT_BEFORE[GROUPS]
    TERMS = ACT_UNITS + 2
    assert TERMS == 17 and P % FIELDS == P - 3 * FIELDS

    TWO_AT = (7, 9)
    XB_SLICE = 2
    L0_TILES = {d: [(0, d - 2)] for d in range(2, 7)} | {7: [(0, 5), (0, 6)]} | {d: [(1, d - 9)] for d in range(9, 16)}
    L0_AT = ((4, 6), (8, 9))
    X1_SLICE = 8
    G_FIRST = 3
    Z2_SLICES, Z2_FROM, Z2_AT_ONCE = (11, 12), 4, 3
    H1_SLICE, H1_AT = 13, (5, 7, 8, 9)
    H2_SLICE = 14
    Y_SLICE, Y_AT = 15, 7
    MID, MOVE_MID = 3, 2
    PAIR_MID, BLOCK_MID, X1_MID, Z0_MID = (1, 5), (4, 7), 5, 8
    QUARTERS = 4

    ctx = ExitStack()
    with ctx:
        def sb(name, shape, dt=f32):
            return ctx.enter_context(nc.sbuf_tensor(name, shape, dt))

        def sem(name):
            return ctx.enter_context(nc.semaphore(name))

        w1_hi = sb("w1_hi", [P, FIELDS * H], f32r)
        w1_lo = sb("w1_lo", [P, FIELDS * H], f32r)
        w2_t = sb("w2_t", [P, FIELDS * H])
        v_t = sb("v_t", [PER_TILE * FIELDS, PAIR_TILES, H])
        wtop1 = sb("wtop1", [P, 4, M1])
        wtop2 = sb("wtop2", [P, M1 // P, M2])
        wtop3 = sb("wtop3", [P, M2 // P])
        btop1 = sb("btop1", [P, M1 // P])
        btop2 = sb("btop2", [P, M2 // P])
        b0_col = sb("b0_col", [P, 1])
        b2_col = sb("b2_col", [P, 1])
        b0_sum = sb("b0_sum", [P, 1])
        b2_sum = sb("b2_sum", [P, 1])
        b1_rows = sb("b1_rows", [P, H])
        ident = sb("ident", [P, P])
        own = sb("own", [P, SAMPLES_PER_G])
        dense_t = sb("dense_t", [DENSE, BATCH])
        ids_sb = sb("ids_sb", [P, CHUNKS, FIELDS], i32)
        idx = sb("idx", [P, FIELDS], i32)
        e_in = sb("e_in", [P, FIELDS, D])
        e_mid = sb("e_mid", [P, 2 * FIELDS, D])
        e_cur = sb("e_cur", [P, FIELDS, D])
        x0_t = sb("x0_t", [2 * FIELDS, COLS])
        x0_rep = sb("x0_rep", [PER_TILE * FIELDS, 2, HALF])
        pairs = sb("pairs", [PER_TILE * FIELDS, SLOTS, HALF])
        x1_hi = sb("x1_hi", [P, COLS], f32r)
        x1_lo = sb("x1_lo", [P, COLS], f32r)
        terms = sb("terms", [P, 2, TERMS, H])
        x2_s = sb("x2_s", [P, D, H])
        x2_r = sb("x2_r", [P, G_GROUPS, H])
        xb = [sb(f"xb{i}", [P, G_GROUPS, FIELDS]) for i in range(3)]
        blocks = sb("blocks", [P, 2, SAMPLES_PER_G, GCOLS])
        g_t = sb("g_t", [P, GCOLS, P])
        z0_part = sb("z0_part", [P, P])
        z0_new = sb("z0_new", [P, P])
        z0_old = sb("z0_old", [P, P])
        z2_sb = sb("z2_sb", [P, P])
        h1_sb = sb("h1_sb", [P, M1 // P, P])
        h2_sb = sb("h2_sb", [P, M2 // P, P])
        y_sb = sb("y_sb", [1, P])
        w12_raw = g_t[:, :, :].rearrange("p j b -> p (j b)")[:, 0:FIELDS * H]
        w0_raw = x2_s[:, :, :].rearrange("p d h -> p (d h)")[:, 0:FIELDS * FIELDS]
        v_raw = x2_r[:, :, :].rearrange("p g h -> p (g h)")[:, 0:SHIFTS * FIELDS]
        dense_raw = terms[:, 0, 0, :].rearrange("p (c e) -> p c e", e=DENSE)

        ring = ctx.enter_context(nc.psum_tensor("ring", [P, RING, BANK], f32))
        l0_ps = ctx.enter_context(nc.psum_tensor("l0_ps", [P, HALF], f32))
        side = ctx.enter_context(nc.psum_tensor("side", [P, 2, BANK], f32))

        y_dram = out.rearrange("b o -> o b")
        x2_dram = nc.dram_tensor("x2_scratch", [D, P, H], f32, kind="Internal").ap()

        w0_in, w1_in, w2_in, ids_in, dense_in, small_in, top_in = (
            sem(n) for n in ("w0_in", "w1_in", "w2_in", "ids_in", "dense_in", "small_in", "top_in"))
        consts_made, zeroed, own_made = sem("consts_made"), sem("zeroed"), sem("own_made")
        bias_sums, v_made = sem("bias_sums"), sem("v_made")
        setup_ps, setup_hi, setup_lo = sem("setup_ps"), sem("setup_hi"), sem("setup_lo")
        idx_ready, gathered, e_cur_ready, e_mid_ready, xb_moved, xb_kept = (
            sem("idx_ready"), sem("gathered"), sem("e_cur_ready"), sem("e_mid_ready"), sem("xb_moved"),
            sem("xb_kept"))
        x0t_ps, x0t_ready, xb_ps, xb_ready = sem("x0t_ps"), sem("x0t_ready"), sem("xb_ps"), sem("xb_ready")
        rep_in = [sem(f"rep_in{half}") for half in range(2)]
        pair_in = [sem(f"pair_in{s}") for s in range(SLOTS)]
        pair_made, pair_used = sem("pair_made"), sem("pair_used")
        x1_hi_ready, x1_lo_ready, z0_summed, z0_ready, z0_kept = (
            sem("x1_hi_ready"), sem("x1_lo_ready"), sem("z0_summed"), sem("z0_ready"), sem("z0_kept"))
        y_group, act_group, dve_unit = sem("y_group"), sem("act_group"), sem("dve_unit")
        folded, x2_done = sem("folded"), sem("x2_done")
        x2_out, x2_in = sem("x2_out"), sem("x2_in")
        block_made, g_ps, g_ready = sem("block_made"), sem("g_ps"), sem("g_ready")
        z2_ps, z2_ready, h1_ps, h1_ready, h2_ps, h2_ready, y_ps, y_ready, y_out = (
            sem(n) for n in ("z2_ps", "z2_ready", "h1_ps", "h1_ready", "h2_ps", "h2_ready", "y_ps", "y_ready",
                             "y_out"))

        block = ctx.enter_context(nc.Block())

        def after(eng, semaphore, count):
            if not isinstance(count, int) or count > 0:
                eng.wait_ge(semaphore, count)

        def steps(eng, step):
            step(-1, first=True, layer1=False, following=True, previous=False, gathers=True)
            step(0, layer1=True, following=True, previous=False, gathers=True)
            with eng.Fori(1, CHUNKS - 2) as c:
                step(c, layer1=True, following=True, previous=True, gathers=True)
            step(CHUNKS - 2, layer1=True, following=True, previous=True, gathers=False)
            step(CHUNKS - 1, layer1=True, following=False, previous=True, gathers=False)
            step(CHUNKS, layer1=False, following=False, previous=True, gathers=False)

        SETUP_W1, SETUP_W2 = GROUPS, GROUPS
        SETUP_V = -(-PAIR_TILES // 4)
        SETUP_DENSE = CHUNKS // 4
        SETUP = SETUP_V + SETUP_DENSE + SETUP_W1 + SETUP_W2

        @block.sync
        def _(sp):
            sp.dma_start(ids_sb[:, :, :], ids.rearrange("(c p) f -> p c f", p=P)).then_inc(ids_in, 16)
            sp.dma_start(w0_raw, W0).then_inc(w0_in, 16)
            sp.dma_start(dense_raw, dense_ctx.rearrange("(c p) e -> p c e", p=P)).then_inc(dense_in, 16)
            sp.dma_start(w12_raw, W1).then_inc(w1_in, 16)
            col = lambda a: a.rearrange("(p o) -> p o", o=1)
            sp.dma_start(b0_col[:, :], col(b0)).then_inc(small_in, 16)
            sp.dma_start(b2_col[:, :], col(b2)).then_inc(small_in, 16)
            sp.dma_start(b1_rows[:, :], b1.rearrange("(o h) -> o h", o=1).to_broadcast([P, H])).then_inc(small_in, 16)
            sp.dma_start(wtop1[:, 0:3, :], W_top1[0:3 * P, :].rearrange("(t p) m -> p t m", p=P)).then_inc(top_in, 16)
            sp.dma_start(wtop1[0:DENSE, 3, :], W_top1[3 * P:, :]).then_inc(top_in, 16)
            sp.dma_start(wtop2[:, :, :], W_top2.rearrange("(t p) m -> p t m", p=P)).then_inc(top_in, 16)
            with nc.allow_non_contiguous_dma(reason="a few hundred words onto the partitions"):
                sp.dma_start(wtop3[:, :], W_top3.rearrange("(t p) o -> p (t o)", p=P)).then_inc(top_in, 16)
                sp.dma_start(btop1[:, :], b_top1.rearrange("(t p) -> p t", p=P)).then_inc(top_in, 16)
                sp.dma_start(btop2[:, :], b_top2.rearrange("(t p) -> p t", p=P)).then_inc(top_in, 16)
            sp.wait_ge(setup_ps, SETUP - SETUP_W2)
            sp.dma_start(w12_raw, W2).then_inc(w2_in, 16)

            def step(c, layer1, following, previous, gathers, first=False):
                def pair_tile(half, t):
                    before = t - SLOTS if t >= SLOTS else (t + SLOTS if t + SLOTS < PAIR_TILES else t) - PAIR_TILES
                    after(sp, pair_used, PAIR_TILES * (2 * (c + 1) + half) + before + 1)
                    for n in range(SHIFTS_OF[t]):
                        s = PER_TILE * t + n
                        sp.dma_start(pairs[n * FIELDS:(n + 1) * FIELDS, t % SLOTS, :],
                                     x0_t[s:s + FIELDS, half * HALF:(half + 1) * HALF]
                                     ).then_inc(pair_in[t % SLOTS], 16)

                def rep(half):
                    after(sp, x0t_ready, 4 * (c + 1) + 2 * half + 2)
                    after(sp, pair_made, PAIR_TILES * (2 * c + half + 1))
                    for n in range(PER_TILE):
                        sp.dma_start(x0_rep[n * FIELDS:(n + 1) * FIELDS, half, :],
                                     x0_t[0:FIELDS, half * HALF:(half + 1) * HALF]).then_inc(rep_in[half], 16)

                def x2_write(chunk, q):
                    n = D // QUARTERS
                    after(sp, x2_done, D * chunk + n * (q + 1))
                    after(sp, x2_in, 16 * chunk)
                    sp.dma_start(x2_dram[n * q:n * (q + 1), :, :].rearrange("d b h -> b d h"),
                                 x2_s[:, n * q:n * (q + 1), :]).then_inc(x2_out, 16)

                if previous:
                    x2_write(c - 1, QUARTERS - 1)
                    after(sp, x2_out, 16 * QUARTERS * c)
                    after(sp, g_ps, G_GROUPS * (c - 1))
                    sp.dma_start(x2_r[:, :, :],
                                 x2_dram.rearrange("d (b g) h -> (d b) g h", g=G_GROUPS)
                                 ).then_inc(x2_in, 16)
                if following:
                    rep(0)
                for half in range(2):
                    for t in range(PAIR_TILES):
                        if following:
                            pair_tile(half, t)
                            if half == 0 and t == SLOTS - 1:
                                rep(1)
                        if layer1 and t == PAIR_TILES // 2 and half == 1:
                            x2_write(c, 1)
                    if layer1:
                        x2_write(c, 2 * half)
                if previous:
                    after(sp, y_ready, c)
                    sp.dma_start(y_dram[:, bass.ds((c - 1) * P, P)], y_sb[0:1, :]).then_inc(y_out, 16)

            steps(sp, step)
            sp.wait_ge(y_out, 16 * CHUNKS)
            sp.wait_ge(x2_out, 16 * QUARTERS * CHUNKS)

        @block.gpsimd
        def _(pool):
            def gather(chunk, f):
                nc.gpsimd.indirect_dma_start(
                    e_in[:, f, :], None, tables[f], bass.IndirectOffsetOnAxis(ap=idx[:, f:f + 1], axis=0)
                ).then_inc(gathered, 16)

            pool.wait_ge(ids_in, 16)
            nc.gpsimd.tensor_copy(idx[:, :], ids_sb[:, 0, :]).then_inc(idx_ready, 1)
            nc.gpsimd.memset(ident[:, :], 0.0).then_inc(zeroed, 1)
            pool.wait_ge(zeroed, 1)
            nc.gpsimd.affine_select(out=ident[:, :], in_=ident[:, :], compare_op=ALU.not_equal, fill=1.0, base=0,
                                    pattern=[[-1, P]], channel_multiplier=1).then_inc(consts_made, 1)
            pool.wait_ge(idx_ready, 1)
            for f in range(FIELDS):
                gather(0, f)

            def step(c, layer1, following, previous, gathers, first=False):
                def next_index():
                    pool.wait_ge(gathered, 16 * FIELDS * (c + 2))
                    nc.gpsimd.tensor_copy(idx[:, :], ids_sb[:, c + 2, :]).then_inc(idx_ready, 1)

                if not layer1:
                    if gathers:
                        next_index()
                        pool.wait_ge(idx_ready, c + 3)
                        pool.wait_ge(e_mid_ready, c + 2)
                        for f in range(FIELDS):
                            gather(c + 2, f)
                    return
                for d in range(D):
                    t = terms[:, d % 2]
                    n = D * c + d
                    after(pool, act_group, len(ACT_GROUPS) * (n + 1))
                    after(pool, dve_unit, DVE_UNITS * (n + 1))
                    if d == 0:
                        after(pool, x2_out, 16 * QUARTERS * c)
                    for i, w in enumerate((8, 4, 2, 1)):
                        nc.gpsimd.tensor_tensor(t[:, 0:w, :], t[:, 0:w, :], t[:, w:2 * w, :],
                                                ALU.add).then_inc(folded, 1)
                        if i == 0 and d == 0 and gathers:
                            next_index()
                            pool.wait_ge(idx_ready, c + 3)
                            pool.wait_ge(e_mid_ready, c + 2)
                        pool.wait_ge(folded, 4 * n + i + 1)
                    nc.gpsimd.tensor_tensor(x2_s[:, d, :], t[:, 0, :], t[:, TERMS - 1, :],
                                            ALU.add).then_inc(x2_done, 1)
                    if gathers:
                        for f in range(3 * d, min(3 * d + 3, FIELDS)):
                            gather(c + 2, f)

            steps(pool, step)

        @block.scalar
        def _(act):
            def setup_copy(batch, dst, rows, width):
                act.wait_ge(setup_ps, batch + 1)
                nc.scalar.activation(dst, ring[0:rows, batch % RING, 0:width], ACT.Copy).then_inc(setup_hi, 1)

            batch = 0
            for q in range(SETUP_V):
                act.wait_ge(setup_ps, batch + 1)
                for i, t in enumerate(range(4 * q, min(4 * q + 4, PAIR_TILES))):
                    rows = ROWS_OF[t]
                    last = nc.scalar.activation(v_t[0:rows, t, :], ring[0:rows, batch % RING, i * H:(i + 1) * H],
                                                ACT.Copy)
                last.then_inc(setup_hi, 1)
                batch += 1
            for q in range(SETUP_DENSE):
                setup_copy(batch, dense_t[:, BANK * q:BANK * (q + 1)], DENSE, BANK)
                batch += 1
            for dst in (w1_hi, w2_t):
                for q in range(GROUPS):
                    n = min(BANK, FIELDS * H - BANK * q)
                    setup_copy(batch, dst[:, BANK * q:BANK * q + n], P, n)
                    batch += 1

            def step(c, layer1, following, previous, gathers, first=False):
                def x1_half(chunk, half):
                    after(act, pair_used, 14 * chunk + 7 * half + 7)
                    after(act, y_group, GROUPS * (D * (chunk - 1) + D // 2 * (half + 1)))
                    nc.scalar.activation(x1_hi[:, half * HALF:(half + 1) * HALF], l0_ps[:, :], ACT.Identity,
                                         bias=b0_col[:, 0:1]).then_inc(x1_hi_ready, 1)

                def move_x0(d):
                    if following and d == 0:
                        after(act, gathered, 16 * FIELDS * (c + 2))
                        after(act, x0t_ps, 4 * (c + 1))
                        after(act, e_cur_ready, c + 1)
                        for i in range(2):
                            last = nc.scalar.activation(e_mid[:, i * FIELDS:(i + 1) * FIELDS, :], e_in[:, :, :],
                                                        ACT.Copy)
                        last.then_inc(e_mid_ready, 1)
                    if d == 1 and previous:
                        after(act, block_made, G_GROUPS * (c - 1))
                        after(act, xb_kept, c)
                        nc.scalar.activation(xb[2][:, :, :], xb[1][:, :, :], ACT.Copy).then_inc(xb_moved, 1)
                    if d == 1 and layer1:
                        after(act, xb_ready, 2 * (c + 1))
                        after(act, xb_moved, c)
                        nc.scalar.activation(xb[1][:, :, :], xb[0][:, :, :], ACT.Copy).then_inc(xb_kept, 1)

                def side_work(d):
                    e = d - 1
                    if following and 0 <= e < 2:
                        for q in (2 * e, 2 * e + 1):
                            after(act, x0t_ps, 4 * (c + 1) + q + 1)
                            for s in range(SLOTS):
                                after(act, pair_in[s], SLOT_COUNT[s] * 2 * (c + 1))
                            for h in range(2):
                                after(act, rep_in[h], 16 * PER_TILE * (c + 1))
                            after(act, xb_ps, 2 * (c + 1))
                            nc.scalar.activation(x0_t[:, q * BANK:(q + 1) * BANK], side[0:2 * FIELDS, q % 2, :],
                                                 ACT.Copy).then_inc(x0t_ready, 1)
                    if following and e == XB_SLICE:
                        n = G_GROUPS // 2
                        for q in range(2):
                            after(act, xb_ps, 2 * (c + 1) + q + 1)
                            after(act, xb_kept, c + 1)
                            nc.scalar.activation(xb[0][:, n * q:n * (q + 1), :], side[:, q, 0:n * FIELDS],
                                                 ACT.Copy).then_inc(xb_ready, 1)
                    if following and d == X1_SLICE:
                        x1_half(c + 1, 0)
                    if previous and G_FIRST <= e < G_FIRST + G_GROUPS // 2:
                        for g in (2 * (e - G_FIRST), 2 * (e - G_FIRST) + 1):
                            n = G_GROUPS * (c - 1) + g
                            after(act, g_ps, n + 1)
                            after(act, h1_ps, c - 1)
                            nc.scalar.activation(
                                g_t[:, :, g::G_GROUPS],
                                side[:, g % 2, 0:SAMPLES_PER_G * GCOLS].rearrange("p (b j) -> p j b", j=GCOLS),
                                ACT.Copy).then_inc(g_ready, 1)
                    if previous and e == 12:
                        after(act, z2_ps, c)
                        after(act, h1_ps, c - 1)
                        nc.scalar.activation(z2_sb[:, :], side[:, 0, 0:P], ACT.Identity,
                                             bias=b2_sum[:, 0:1]).then_inc(z2_ready, 1)
                    if previous and e == H1_SLICE:
                        after(act, h1_ps, c)
                        after(act, h2_ps, c - 1)
                        for m in range(M1 // P):
                            last = nc.scalar.activation(h1_sb[:, m, :], side[:, 1, m * P:(m + 1) * P], ACT.Relu,
                                                        bias=btop1[:, m:m + 1])
                        last.then_inc(h1_ready, 1)
                    if previous and e == H2_SLICE:
                        after(act, h2_ps, c)
                        after(act, y_ps, c - 1)
                        for m in range(M2 // P):
                            last = nc.scalar.activation(h2_sb[:, m, :], side[:, 0, m * P:(m + 1) * P], ACT.Relu,
                                                        bias=btop2[:, m:m + 1])
                        last.then_inc(h2_ready, 1)

                for d in range(D):
                    if not layer1:
                        move_x0(d)
                        side_work(d)
                        continue
                    n = D * c + d
                    if d == 0:
                        act.wait_ge(e_cur_ready, c + 1)
                    after(act, x2_done, n - 1)
                    for g in range(GROUPS):
                        if g == MID:
                            side_work(d)
                            if d == 0:
                                x1_half(c, 1)
                        if g == MOVE_MID:
                            move_x0(d)
                        if g not in ACT_GROUPS:
                            continue
                        after(act, y_group, GROUPS * n + g + 1)
                        for i in range(WIDTH[g]):
                            j = GROUP * g + i
                            last = nc.scalar.activation(terms[:, d % 2, ACT_BEFORE[g] + i, :],
                                                        ring[:, (GROUPS * d + g) % RING, i * H:(i + 1) * H], ACT.Copy,
                                                        scale=e_cur[:, j, d:d + 1])
                        last.then_inc(act_group, 1)
                if previous:
                    if not layer1:
                        side_work(D)
                    after(act, y_ps, c)
                    after(act, y_out, 16 * (c - 1))
                    nc.scalar.activation(y_sb[0:1, :], side[0:1, 1, 0:P], ACT.Copy).then_inc(y_ready, 1)

            act.wait_ge(small_in, 48)
            act.wait_ge(bias_sums, 2)
            act.wait_ge(top_in, 96)
            steps(act, step)

        @block.vector
        def _(dve):
            dve.wait_ge(w0_in, 16)
            nc.vector.tensor_copy(v_raw[:, 0:FIELDS], w0_raw[:, 0:FIELDS * FIELDS:FIELDS + 1])
            for s in range(1, SHIFTS):
                for i0, i1, a, b in ((0, FIELDS - s, s, FIELDS * s),
                                     (FIELDS - s, FIELDS, s - FIELDS, FIELDS * (s - FIELDS))):
                    step40 = FIELDS + 1
                    n = i1 - i0
                    x = step40 * i0 + a
                    y = step40 * i0 + b
                    last = nc.vector.tensor_tensor(
                        v_raw[:, s * FIELDS + i0:s * FIELDS + i1],
                        w0_raw[:, x:x + step40 * (n - 1) + 1:step40],
                        w0_raw[:, y:y + step40 * (n - 1) + 1:step40], ALU.add)
            last.then_inc(v_made, 1)
            dve.wait_ge(small_in, 48)
            nc.vector.tensor_scalar(b0_sum[:, :], b0_col[:, :], float(D), None, ALU.mult).then_inc(bias_sums, 1)
            nc.vector.tensor_scalar(b2_sum[:, :], b2_col[:, :], float(D), None, ALU.mult).then_inc(bias_sums, 1)
            dve.wait_ge(consts_made, 1)
            nc.vector.tensor_reduce(own[:, :], ident[:, :].rearrange("p (d b) -> p b d", d=D), AX.X,
                                    ALU.add).then_inc(own_made, 1)
            dve.wait_ge(own_made, 1)
            for i in range(2):
                nc.vector.tensor_copy(blocks[:, i, :, FIELDS], own[:, :])
            for q in range(GROUPS):
                batch = SETUP_V + SETUP_DENSE + q
                n = min(BANK, FIELDS * H - BANK * q)
                dve.wait_ge(setup_hi, batch + 1)
                nc.vector.tensor_tensor(w1_lo[:, BANK * q:BANK * q + n], ring[:, batch % RING, 0:n],
                                        w1_hi[:, BANK * q:BANK * q + n].bitcast(f32),
                                        ALU.subtract).then_inc(setup_lo, 1)

            def step(c, layer1, following, previous, gathers, first=False):
                def x1_lower(chunk, half):
                    x = slice(half * HALF, (half + 1) * HALF)
                    after(dve, x1_hi_ready, 2 * chunk + half + 1)
                    nc.vector.scalar_tensor_tensor(out=x1_lo[:, x], in0=l0_ps[:, :], scalar=b0_col[:, 0:1],
                                                   in1=x1_hi[:, x].bitcast(f32), op0=ALU.add,
                                                   op1=ALU.subtract).then_inc(x1_lo_ready, 1)

                def z0_half(chunk, half):
                    dst = z0_part if half == 0 else z0_new
                    if half == 1 and not (isinstance(chunk, int) and chunk == 0):
                        after(dve, h1_ps, chunk - 1)
                        nc.vector.tensor_copy(z0_old[:, :], z0_new[:, :]).then_inc(z0_kept, 1)
                        dve.wait_ge(z0_kept, chunk)
                    nc.vector.tensor_reduce(dst[:, :], l0_ps[:, :].rearrange("p (d b) -> p b d", b=P),
                                            AX.X, ALU.add).then_inc(z0_summed, 1)
                    if half == 1:
                        after(dve, z0_summed, 2 * chunk + 2)
                        nc.vector.scalar_tensor_tensor(out=z0_new[:, :], in0=z0_part[:, :], scalar=b0_sum[:, 0:1],
                                                       in1=z0_new[:, :], op0=ALU.add,
                                                       op1=ALU.add).then_inc(z0_ready, 1)

                def make_block(d, i):
                    if previous and G_FIRST <= d < G_FIRST + G_GROUPS // 2:
                        g = 2 * (d - G_FIRST) + i
                        if g == 0:
                            after(dve, xb_moved, c)
                        n = G_GROUPS * (c - 1) + g
                        after(dve, g_ps, n - g if g < 2 else n - 1)
                        shape = [P, SAMPLES_PER_G, FIELDS]
                        nc.vector.tensor_tensor(
                            blocks[:, g % 2, :, 0:FIELDS],
                            xb[2][:, g:g + 1, :].to_broadcast(shape),
                            own[:, :].unsqueeze(2).to_broadcast(shape), ALU.mult).then_inc(block_made, 1)

                def side_work(d, g):
                    if g in BLOCK_MID:
                        make_block(d, BLOCK_MID.index(g))
                    if following and g in PAIR_MID and PAIR_MID.index(g) < len(L0_TILES.get(d, ())):
                        half, t = L0_TILES[d][PAIR_MID.index(g)]
                        rows = ROWS_OF[t]
                        s = t % SLOTS
                        k = 2 * (c + 1) + half
                        after(dve, rep_in[half], 16 * PER_TILE * (c + 2))
                        after(dve, pair_in[s], SLOT_COUNT[s] * k + 16 * sum(SHIFTS_OF[s:t + 1:SLOTS]))
                        nc.vector.tensor_tensor(pairs[0:rows, s, :], x0_rep[0:rows, half, :], pairs[0:rows, s, :],
                                                ALU.mult).then_inc(pair_made, 1)
                    if following and d == X1_SLICE:
                        if g == X1_MID:
                            x1_lower(c + 1, 0)
                        if g == Z0_MID:
                            z0_half(c + 1, 0)
                    if layer1 and d == 0 and g == X1_MID:
                        x1_lower(c, 1)
                    if layer1 and d == 1 and g == X1_MID:
                        z0_half(c, 1)

                if layer1:
                    after(dve, act_group, len(ACT_GROUPS) * D * c)
                    after(dve, dve_unit, DVE_UNITS * D * c)
                    after(dve, e_mid_ready, c + 1)
                    nc.vector.tensor_copy(e_cur[:, :, :], e_mid[:, 0:FIELDS, :]).then_inc(e_cur_ready, 1)
                    dve.wait_ge(e_cur_ready, c + 1)
                for d in range(D):
                    n = D * c + d
                    if layer1:
                        after(dve, x2_done, n - 1)
                    unit = 0
                    for g in range(GROUPS):
                        side_work(d, g)
                        if not layer1:
                            continue
                        if g in ACT_GROUPS:
                            continue
                        after(dve, y_group, GROUPS * n + g + 1)
                        for i in range(WIDTH[g]):
                            j = GROUP * g + i
                            y = ring[:, (GROUPS * d + g) % RING, i * H:(i + 1) * H]
                            acc = terms[:, d % 2, ACT_UNITS + unit % 2, :]
                            if unit == 0:
                                nc.vector.scalar_tensor_tensor(out=acc, in0=y, scalar=e_cur[:, j, d:d + 1],
                                                               in1=b1_rows[:, :], op0=ALU.mult,
                                                               op1=ALU.add).then_inc(dve_unit, 1)
                            elif unit == 1:
                                nc.vector.tensor_scalar(acc, y, e_cur[:, j, d:d + 1], None,
                                                        ALU.mult).then_inc(dve_unit, 1)
                            else:
                                after(dve, dve_unit, DVE_UNITS * n + unit - 1)
                                nc.vector.scalar_tensor_tensor(out=acc, in0=y, scalar=e_cur[:, j, d:d + 1],
                                                               in1=acc, op0=ALU.mult,
                                                               op1=ALU.add).then_inc(dve_unit, 1)
                            unit += 1

            steps(dve, step)

        @block.tensor
        def _(pe):
            pe.wait_ge(consts_made, 1)
            batch = 0

            def bank_free(batch):
                after(pe, setup_hi, batch - RING + 1)
                after(pe, setup_lo, min(batch - RING + 1 - SETUP_V - SETUP_DENSE, SETUP_W1))

            pe.wait_ge(v_made, 1)
            for q in range(SETUP_V):
                bank_free(batch)
                for i, t in enumerate(range(4 * q, min(4 * q + 4, PAIR_TILES))):
                    x = PER_TILE * FIELDS * t
                    rows = ROWS_OF[t]
                    last = nc.tensor.transpose(ring[0:rows, batch % RING, i * H:(i + 1) * H], v_raw[:, x:x + rows],
                                               ident[:, :])
                last.then_inc(setup_ps, 1)
                batch += 1
            pe.wait_ge(dense_in, 16)
            for q in range(SETUP_DENSE):
                bank_free(batch)
                for i in range(4):
                    last = nc.tensor.transpose(ring[0:DENSE, batch % RING, i * P:(i + 1) * P],
                                               dense_raw[:, 4 * q + i, :], ident[:, :])
                last.then_inc(setup_ps, 1)
                batch += 1
            for loaded in (w1_in, w2_in):
                pe.wait_ge(loaded, 16)
                for q in range(GROUPS):
                    bank_free(batch)
                    for i, j in enumerate(range(GROUP * q, min(GROUP * (q + 1), FIELDS))):
                        last = nc.tensor.transpose(ring[:, batch % RING, i * H:(i + 1) * H],
                                                   w12_raw[:, j * H:(j + 1) * H], ident[:, :])
                    last.then_inc(setup_ps, 1)
                    batch += 1

            def step(c, layer1, following, previous, gathers, first=False):
                def layer0(half, t, x):
                    rows = ROWS_OF[t]
                    n = 2 * (c + 1) + half
                    if x == 0:
                        if t == 0:
                            after(pe, x1_hi_ready, n)
                            after(pe, x1_lo_ready, n)
                            after(pe, z0_summed, n)
                        after(pe, pair_made, PAIR_TILES * n + t + 1)
                    last = nc.tensor.matmul(l0_ps[:, x:x + BANK], v_t[0:rows, t, :],
                                            pairs[0:rows, t % SLOTS, x:x + BANK],
                                            start=(t == 0), stop=(t == PAIR_TILES - 1))
                    if x:
                        last.then_inc(pair_used, 1)

                def side_work(d, g):
                    if following and d < 2 and g in TWO_AT:
                        if d == 0 and g == TWO_AT[0]:
                            after(pe, h2_ready, c - 1)
                            after(pe, y_ready, c - 1)
                            after(pe, e_mid_ready, c + 2)
                        q = 2 * d + TWO_AT.index(g)
                        after(pe, x0t_ready, 4 * (c + 1) + q - 1)
                        for i in range(4):
                            last = nc.tensor.transpose(side[0:2 * FIELDS, q % 2, i * P:(i + 1) * P],
                                                       e_mid[:, :, 4 * q + i], ident[:, :])
                        last.then_inc(x0t_ps, 1)
                    if following and d == XB_SLICE and g in TWO_AT:
                        if not layer1:
                            after(pe, x0t_ready, 4 * (c + 1) + 4)
                        q = TWO_AT.index(g)
                        n = G_GROUPS // 2
                        for i in range(n):
                            r = q * n + i
                            last = nc.tensor.transpose(side[:, q, i * FIELDS:(i + 1) * FIELDS],
                                                       x0_t[0:FIELDS, r::G_GROUPS],
                                                       ident[0:FIELDS, 0:FIELDS])
                        last.then_inc(xb_ps, 1)
                    if previous and G_FIRST <= d < G_FIRST + G_GROUPS // 2 and g in TWO_AT:
                        r = 2 * (d - G_FIRST) + TWO_AT.index(g)
                        if r == 0:
                            if not (isinstance(c, int) and c >= CHUNKS - 1):
                                after(pe, xb_ready, 2 * (c + 2))
                            after(pe, h2_ready, c - 1)
                            after(pe, y_ready, c - 1)
                            after(pe, x2_in, 16 * c)
                        n = G_GROUPS * (c - 1) + r
                        after(pe, block_made, n + 1)
                        if r >= 2:
                            after(pe, g_ready, n - 1)
                        nc.tensor.matmul(side[:, r % 2, 0:SAMPLES_PER_G * GCOLS], x2_r[:, r, :],
                                         blocks[:, r % 2, :, :].rearrange("p b j -> p (b j)"),
                                         start=True, stop=True).then_inc(g_ps, 1)
                    if previous and d in Z2_SLICES:
                        j0 = Z2_AT_ONCE * (GROUPS * Z2_SLICES.index(d) + g - Z2_FROM)
                        if j0 == 0:
                            after(pe, g_ready, G_GROUPS * c)
                        for j in range(max(j0, 0), min(j0 + Z2_AT_ONCE, FIELDS)):
                            last = nc.tensor.matmul(side[:, 0, 0:P], w2_t[:, j * H:(j + 1) * H], g_t[:, j, :],
                                                    start=(j == 0), stop=(j == FIELDS - 1))
                            if j == FIELDS - 1:
                                last.then_inc(z2_ps, 1)
                    if previous and d == H1_SLICE and g in H1_AT:
                        m = H1_AT.index(g)
                        if m == 0:
                            after(pe, z2_ready, c)
                            after(pe, z0_ready, c)
                            if layer1:
                                after(pe, z0_kept, c)
                        z0 = z0_old if layer1 else z0_new
                        for k, z in enumerate((z0[:, :], g_t[:, FIELDS, :], z2_sb[:, :],
                                               dense_t[:, bass.ds((c - 1) * P, P)])):
                            rows = DENSE if k == 3 else P
                            last = nc.tensor.matmul(side[:, 1, m * P:(m + 1) * P],
                                                    wtop1[0:rows, k, m * P:(m + 1) * P], z,
                                                    start=(k == 0), stop=(k == 3))
                        if m == M1 // P - 1:
                            last.then_inc(h1_ps, 1)
                    if previous and d == H2_SLICE and g in TWO_AT:
                        after(pe, h1_ready, c)
                        m = TWO_AT.index(g)
                        for k in range(M1 // P):
                            last = nc.tensor.matmul(side[:, 0, m * P:(m + 1) * P],
                                                    wtop2[:, k, m * P:(m + 1) * P], h1_sb[:, k, :],
                                                    start=(k == 0), stop=(k == M1 // P - 1))
                        if m == M2 // P - 1:
                            last.then_inc(h2_ps, 1)
                    if previous and d == Y_SLICE and g == Y_AT:
                        after(pe, h2_ready, c)
                        for k in range(M2 // P):
                            last = nc.tensor.matmul(side[0:1, 1, 0:P], wtop3[:, k:k + 1], h2_sb[:, k, :],
                                                    start=(k == 0), stop=(k == M2 // P - 1))
                        last.then_inc(y_ps, 1)
                    if following:
                        for (half, t), at in zip(L0_TILES.get(d, ()), L0_AT):
                            if g in at:
                                layer0(half, t, at.index(g) * BANK)

                for d in range(D):
                    if layer1 and d % (D // 2) == 0:
                        k = 2 * c + d // (D // 2) + 1
                        after(pe, x1_hi_ready, k)
                        after(pe, x1_lo_ready, k)
                    x = slice(d * P, (d + 1) * P)
                    for g in range(GROUPS):
                        if layer1:
                            width = WIDTH[g] * H
                            w = slice(g * BANK, g * BANK + width)
                            if following and d == XB_SLICE and g == TWO_AT[0]:
                                after(pe, x0t_ready, 4 * (c + 1) + 4)
                            slice_before, b = (D * c + d, g - RING) if g >= RING else (D * c + d - 1, g - RING + GROUPS)
                            if b in ACT_GROUPS:
                                after(pe, act_group, len(ACT_GROUPS) * slice_before
                                      + sum(h <= b for h in ACT_GROUPS))
                            else:
                                after(pe, dve_unit, DVE_UNITS * slice_before + DVE_BEFORE[b + 1])
                            acc = ring[:, (GROUPS * d + g) % RING, 0:width]
                            nc.tensor.matmul(acc, x1_hi[:, x], w1_hi[:, w], start=True, stop=False)
                            nc.tensor.matmul(acc, x1_hi[:, x], w1_lo[:, w], start=False, stop=False)
                            nc.tensor.matmul(acc, x1_lo[:, x], w1_hi[:, w], start=False,
                                             stop=True).then_inc(y_group, 1)
                        side_work(d, g)

            pe.wait_ge(top_in, 96)
            pe.wait_ge(setup_hi, SETUP)
            pe.wait_ge(setup_lo, SETUP_W1)
            steps(pe, step)


_TABLES = [f"tbl_{f}" for f in range(TABLES)]
_INS = (["dense_ctx", "ids"] + _TABLES + ["W_top1", "b_top1", "W_top2", "b_top2", "W_top3"]
        + [f"L0_rec_{kind}{layer}" for layer in range(3) for kind in "Wb"])


def kernel(**inputs):
    import numpy as _np
    import concourse.bacc as _bacc
    from concourse import mybir as _mybir
    from concourse.bass_utils import run_bass_kernel_spmd as _run

    nc = _bacc.Bacc("TRN2", target_bir_lowering=False, num_devices=1)
    arrays, aps = {}, {}
    for name in _INS:
        a = _np.ascontiguousarray(inputs[name])
        arrays[f"in_{name}"] = a
        aps[name] = nc.dram_tensor(f"in_{name}", a.shape, _mybir.dt.from_np(a.dtype), kind="ExternalInput").ap()
    batch = arrays["in_ids"].shape[0]
    out = nc.dram_tensor("out_y", (batch, 1), _mybir.dt.float32, kind="ExternalOutput").ap()
    build_tower(nc, aps["dense_ctx"], aps["ids"], [aps[t] for t in _TABLES], aps["W_top1"], aps["b_top1"],
                aps["W_top2"], aps["b_top2"], aps["W_top3"], aps["L0_rec_W0"], aps["L0_rec_b0"], aps["L0_rec_W1"],
                aps["L0_rec_b1"], aps["L0_rec_W2"], aps["L0_rec_b2"], out)
    return _run(nc, [arrays], core_ids=[0]).results[0]["out_y"]
```

```python
import concourse.bass as bass
from concourse import mybir
from contextlib import ExitStack

FIELDS, D, H = 39, 16, 128
P = 128
TABLES = FIELDS


def build_tower(nc, dense_ctx, ids, tables, W_top1, b_top1, W_top2, b_top2, W_top3, W0, b0, W1, b1, W2, b2, out):
    f32, f32r, i32 = mybir.dt.float32, mybir.dt.float32r, mybir.dt.int32
    ALU = mybir.AluOpType
    ACT = mybir.ActivationFunctionType
    AX = mybir.AxisListType

    BATCH = ids.shape[0]
    CHUNKS = BATCH // P
    COLS = D * P
    HALF = COLS // 2
    SHIFTS = FIELDS // 2 + 1
    PER_TILE = P // FIELDS
    PAIR_TILES = -(-SHIFTS // PER_TILE)
    SHIFTS_OF = [min(PER_TILE, SHIFTS - PER_TILE * t) for t in range(PAIR_TILES)]
    ROWS_OF = [n * FIELDS for n in SHIFTS_OF]
    FIRST_SLOTS = 4
    BANK = 512
    GROUP = BANK // H
    GROUPS = -(-FIELDS // GROUP)
    TILES = 2 * PAIR_TILES
    TILE = [(half, t) for half in range(2) for t in range(PAIR_TILES)]
    SLOT_BEFORE = [16 * sum(SHIFTS_OF[TILE[k][1]] for k in range(i % 2, i, 2)) for i in range(TILES + 2)]
    RING = 4
    SAMPLES_PER_G = P // D
    G_GROUPS = P // SAMPLES_PER_G
    GCOLS = FIELDS + 1
    M1, M2 = W_top1.shape[1], W_top2.shape[1]
    DENSE = dense_ctx.shape[1]

    ACT_GROUPS = [(1, 3, 5, 7, 9) if 6 <= d <= 13 or d in (0, 15) else (1, 3, 6, 8) for d in range(D)]
    WIDTH = [min(GROUP, FIELDS - GROUP * g) for g in range(GROUPS)]
    ACT_BEFORE = [[sum(WIDTH[h] for h in range(g) if h in ACT_GROUPS[d]) for g in range(GROUPS + 1)]
                  for d in range(D)]
    DVE_BEFORE = [[sum(WIDTH[:g]) - ACT_BEFORE[d][g] for g in range(GROUPS + 1)] for d in range(D)]
    TERMS = [ACT_BEFORE[d][GROUPS] + 2 for d in range(D)]
    FOLDS = {21: (21, 11, 6, 3), 18: (18, 9, 5, 3)}

    def scaled(c, d, g):
        if d < 0:
            c, d = c - 1, d + D
        return (sum(len(a) for a in ACT_GROUPS) * c + sum(len(a) for a in ACT_GROUPS[:d])
                + sum(h <= g for h in ACT_GROUPS[d]))

    def summed(c, d, fields):
        if d < 0:
            c, d = c - 1, d + D
        return sum(v[GROUPS] for v in DVE_BEFORE) * c + sum(v[GROUPS] for v in DVE_BEFORE[:d]) + fields

    TWO_AT = (6, 9)
    Z2_SLICES, Z2_FROM, Z2_AT_ONCE = (0, 1, 2), 4, 2
    XB_SLICES, XB_AT = (0, 1), 6
    DENSE_SLICE = 2
    H1_SLICE, H1_AT = 3, (6, 7, 8, 9)
    H2_SLICE = 4
    Y_SLICE, Y_AT = 5, 7
    MOVE_SLICE = 5
    X0T_SLICES = (6, 7)
    G_FIRST = 8
    TILES_MADE = {0: [7], 1: [8, 9], 2: [10], 3: [11], 4: [12], 5: [13],
                  8: [None, 0], 9: [1], 10: [2], 11: [3], 12: [4, 5], 13: [None, 6]}
    L0_AT = ((3, 5), (7, 8))
    X1_HI_AT = {1: (6, 7), 0: (15, 2)}
    X1_LO_AT = {1: (7, 1), 0: (15, 4)}
    Z0_AT = {1: (7, 7), 0: (15, 9)}
    MID, MOVE_MID, HI_MID = 3, 2, (5, 9)
    MADE_MID, LO_MID, BLOCK_MID = (1, 6), ((0, 9), (1, 3)), (3, 5)
    GATHERS = (3, 4, 4, 3, 0, 0, 2, 2, 2, 2, 2, 2, 2, 2, 4, 5)
    INDEX_SLICE = 6
    LATE = sum(GATHERS[:INDEX_SLICE])
    assert sum(GATHERS) == FIELDS
    LO_MID_FIRST = ((1, 2), (1, 7))
    X2_WRITES = {13: 0, 3: 1, 6: 2}
    X2_LAST_AFTER = 9
    X2_SLOTS = 8
    QUARTERS = 4

    ctx = ExitStack()
    with ctx:
        def sb(name, shape, dt=f32):
            return ctx.enter_context(nc.sbuf_tensor(name, shape, dt))

        def sem(name):
            return ctx.enter_context(nc.semaphore(name))

        w1_hi = sb("w1_hi", [P, FIELDS * H], f32r)
        w1_lo = sb("w1_lo", [P, FIELDS * H], f32r)
        w2_t = sb("w2_t", [P, FIELDS * H])
        v_hi = sb("v_hi", [PER_TILE * FIELDS, PAIR_TILES, H], f32r)
        v_lo = sb("v_lo", [PER_TILE * FIELDS, PAIR_TILES, H], f32r)
        wtop1 = sb("wtop1", [P, 4, M1])
        wtop2 = sb("wtop2", [P, M1 // P, M2])
        wtop3 = sb("wtop3", [P, M2 // P])
        btop1 = sb("btop1", [P, M1 // P])
        btop2 = sb("btop2", [P, M2 // P])
        b0_col = sb("b0_col", [P, 1])
        b2_col = sb("b2_col", [P, 1])
        b0_sum = sb("b0_sum", [P, 1])
        b2_sum = sb("b2_sum", [P, 1])
        b1_rows = sb("b1_rows", [P, H])
        ident = sb("ident", [P, P])
        own = sb("own", [P, SAMPLES_PER_G])
        ids_sb = sb("ids_sb", [P, CHUNKS, FIELDS], i32)
        idx = sb("idx", [P, FIELDS], i32)
        e_in = sb("e_in", [P, FIELDS, D])
        e_mid = sb("e_mid", [P, 2 * FIELDS, D])
        e_cur = sb("e_cur", [P, FIELDS, D])
        x0_t = sb("x0_t", [2 * FIELDS, COLS])
        x0_rep = sb("x0_rep", [PER_TILE * FIELDS, HALF])
        pairs = sb("pairs", [PER_TILE * FIELDS, 2, HALF])
        pairs_hi = sb("pairs_hi", [PER_TILE * FIELDS, 2, HALF], f32r)
        pairs_lo = sb("pairs_lo", [PER_TILE * FIELDS, 2, HALF], f32r)
        x1_hi = sb("x1_hi", [P, COLS], f32r)
        x1_lo = sb("x1_lo", [P, COLS], f32r)
        terms = sb("terms", [P, 2, max(TERMS), H])
        x2_s = sb("x2_s", [P, X2_SLOTS, H])
        x2_r = sb("x2_r", [P, G_GROUPS, H])
        xb = [sb(f"xb{i}", [P, G_GROUPS, FIELDS]) for i in range(2)]
        blocks = sb("blocks", [P, 2, SAMPLES_PER_G, GCOLS])
        g_t = sb("g_t", [P, GCOLS, P])
        z0_part = sb("z0_part", [P, P])
        z0_new = sb("z0_new", [P, P])
        z0_old = sb("z0_old", [P, P])
        dense_raw = sb("dense_raw", [P, DENSE])
        y_sb = sb("y_sb", [P, CHUNKS])
        z2_sb = g_t[:, 0, :]
        dense_t = g_t[0:DENSE, 1, :]
        h2_sb = g_t[:, 2:2 + M2 // P, :]
        h1_sb = g_t[:, 4:4 + M1 // P, :]
        w12_raw = g_t[:, :, :].rearrange("p j b -> p (j b)")[:, 0:FIELDS * H]
        w0_raw = x2_r[:, :, :].rearrange("p g h -> p (g h)")[:, 0:FIELDS * FIELDS]
        more_pairs = x2_r[:, :, :].rearrange("p (s g) h -> p s (g h)", s=2)[0:PER_TILE * FIELDS, :, :]
        v_raw = x2_s[:, :, :].rearrange("p d h -> p (d h)")[:, 0:SHIFTS * FIELDS]

        ring = ctx.enter_context(nc.psum_tensor("ring", [P, RING, BANK], f32))
        l0_ps = ctx.enter_context(nc.psum_tensor("l0_ps", [P, HALF], f32))
        side = ctx.enter_context(nc.psum_tensor("side", [P, 2, BANK], f32))

        def pair_slot(chunk, i):
            if isinstance(chunk, int) and chunk == 0 and i < PAIR_TILES:
                s = i % FIRST_SLOTS
                count = sum(16 * SHIFTS_OF[k] for k in range(s, i + 1, FIRST_SLOTS))
                return pairs[:, s, :] if s < 2 else more_pairs[:, s - 2, :], pair_in[s], count
            s = i % 2
            return (pairs[:, s, :], pair_in[s],
                    loads(chunk, s) + SLOT_BEFORE[i] + 16 * SHIFTS_OF[TILE[i][1]])

        def loads(chunk, s):
            elsewhere = sum(16 * SHIFTS_OF[i] for i in range(PAIR_TILES) if i % 2 == s and i % FIRST_SLOTS >= 2)
            return SLOT_BEFORE[TILES + s] * chunk - elsewhere

        y_dram = out.rearrange("(c p) o -> p (c o)", p=P)
        x2_dram = nc.dram_tensor("x2_scratch", [D, P, H], f32, kind="Internal").ap()

        w0_in, w1_in, w2_in, ids_in, dense_in, small_in, top_in = (
            sem(n) for n in ("w0_in", "w1_in", "w2_in", "ids_in", "dense_in", "small_in", "top_in"))
        consts_made, zeroed, own_made = sem("consts_made"), sem("zeroed"), sem("own_made")
        bias_sums, v_made = sem("bias_sums"), sem("v_made")
        setup_ps, setup_hi, setup_lo = sem("setup_ps"), sem("setup_hi"), sem("setup_lo")
        idx_ready, gathered, e_cur_ready, e_mid_ready, xb_moved = (
            sem("idx_ready"), sem("gathered"), sem("e_cur_ready"), sem("e_mid_ready"), sem("xb_moved"))
        x0t_ps, x0t_ready, xb_ps, xb_ready = sem("x0t_ps"), sem("x0t_ready"), sem("xb_ps"), sem("xb_ready")
        rep_in = sem("rep_in")
        pair_in = [sem(f"pair_in{s}") for s in range(FIRST_SLOTS)]
        pair_made, pair_hi, pair_lo, pair_used = sem("pair_made"), sem("pair_hi"), sem("pair_lo"), sem("pair_used")
        x1_hi_ready, x1_lo_ready, z0_summed, z0_ready, z0_kept = (
            sem("x1_hi_ready"), sem("x1_lo_ready"), sem("z0_summed"), sem("z0_ready"), sem("z0_kept"))
        y_group, act_group, dve_unit = sem("y_group"), sem("act_group"), sem("dve_unit")
        folded, x2_done = sem("folded"), sem("x2_done")
        x2_out = [sem(f"x2_out{i}") for i in range(2)]
        x2_in = sem("x2_in")
        dense_ps, dense_ready = sem("dense_ps"), sem("dense_ready")
        block_made, g_ps, g_ready = sem("block_made"), sem("g_ps"), sem("g_ready")
        z2_ps, z2_ready, h1_ps, h1_ready, h2_ps, h2_ready, y_ps, y_ready, y_out = (
            sem(n) for n in ("z2_ps", "z2_ready", "h1_ps", "h1_ready", "h2_ps", "h2_ready", "y_ps", "y_ready",
                             "y_out"))

        block = ctx.enter_context(nc.Block())

        def after(eng, semaphore, count):
            if not isinstance(count, int) or count > 0:
                eng.wait_ge(semaphore, count)

        def steps(eng, step):
            step(-1, layer1=False, following=True, previous=False, mlp=False, gathers=True)
            step(0, layer1=True, following=True, previous=False, mlp=False, gathers=True)
            step(1, layer1=True, following=True, previous=True, mlp=False, gathers=True)
            with eng.Fori(2, CHUNKS - 2) as c:
                step(c, layer1=True, following=True, previous=True, mlp=True, gathers=True)
            step(CHUNKS - 2, layer1=True, following=True, previous=True, mlp=True, gathers=False)
            step(CHUNKS - 1, layer1=True, following=False, previous=True, mlp=True, gathers=False)
            step(CHUNKS, layer1=False, following=False, previous=True, mlp=True, gathers=False)
            step(CHUNKS + 1, layer1=False, following=False, previous=False, mlp=True, gathers=False)

        def tiles_made(c, d, layer1, following):
            if d < D // 2:
                return [(c, i) for i in TILES_MADE.get(d, ())] if layer1 else []
            return [(c + 1, i) for i in TILES_MADE.get(d, ())] if following else []

        def halves(c, layer1, following):
            return [(1, c)] * layer1 + [(0, c + 1)] * following

        SETUP_W1, SETUP_W2 = GROUPS, GROUPS
        SETUP_V = -(-PAIR_TILES // 4)
        SETUP = SETUP_V + SETUP_W1 + SETUP_W2

        @block.sync
        def _(sp):
            sp.dma_start(ids_sb[:, :, :], ids.rearrange("(c p) f -> p c f", p=P)).then_inc(ids_in, 16)
            sp.dma_start(w0_raw, W0).then_inc(w0_in, 16)
            sp.dma_start(w12_raw, W1).then_inc(w1_in, 16)
            col = lambda a: a.rearrange("(p o) -> p o", o=1)
            sp.dma_start(b0_col[:, :], col(b0)).then_inc(small_in, 16)
            sp.dma_start(b2_col[:, :], col(b2)).then_inc(small_in, 16)
            sp.dma_start(b1_rows[:, :], b1.rearrange("(o h) -> o h", o=1).to_broadcast([P, H])).then_inc(small_in, 16)
            sp.dma_start(wtop1[:, 0:3, :], W_top1[0:3 * P, :].rearrange("(t p) m -> p t m", p=P)).then_inc(top_in, 16)
            sp.dma_start(wtop1[0:DENSE, 3, :], W_top1[3 * P:, :]).then_inc(top_in, 16)
            sp.dma_start(wtop2[:, :, :], W_top2.rearrange("(t p) m -> p t m", p=P)).then_inc(top_in, 16)
            with nc.allow_non_contiguous_dma(reason="a few hundred words onto the partitions"):
                sp.dma_start(wtop3[:, :], W_top3.rearrange("(t p) o -> p (t o)", p=P)).then_inc(top_in, 16)
                sp.dma_start(btop1[:, :], b_top1.rearrange("(t p) -> p t", p=P)).then_inc(top_in, 16)
                sp.dma_start(btop2[:, :], b_top2.rearrange("(t p) -> p t", p=P)).then_inc(top_in, 16)
            sp.wait_ge(setup_ps, SETUP - SETUP_W2)
            sp.dma_start(w12_raw, W2).then_inc(w2_in, 16)

            def step(c, layer1, following, previous, mlp, gathers):
                def pair_tile(chunk, i):
                    half, t = TILE[i]
                    products, loaded, _ = pair_slot(chunk, i)
                    if isinstance(chunk, int) and chunk == 0 and i < PAIR_TILES:
                        after(sp, pair_lo, i - FIRST_SLOTS + 1)
                        after(sp, v_made, 1)
                    else:
                        after(sp, pair_lo, TILES * chunk + i - 1)
                    for n in range(SHIFTS_OF[t]):
                        s = PER_TILE * t + n
                        sp.dma_start(products[n * FIELDS:(n + 1) * FIELDS, :],
                                     x0_t[s:s + FIELDS, half * HALF:(half + 1) * HALF]).then_inc(loaded, 16)

                def rep(chunk, half):
                    after(sp, x0t_ready, 4 * chunk + 2 * half + 2)
                    after(sp, pair_made, PAIR_TILES * (2 * chunk + half))
                    for n in range(PER_TILE):
                        sp.dma_start(x0_rep[n * FIELDS:(n + 1) * FIELDS, :],
                                     x0_t[0:FIELDS, half * HALF:(half + 1) * HALF]).then_inc(rep_in, 16)

                def x2_write(chunk, q):
                    n = D // QUARTERS
                    after(sp, x2_done, D * chunk + n * (q + 1))
                    after(sp, x2_in, 16 * chunk)
                    x = n * q % X2_SLOTS
                    sp.dma_start(x2_dram[n * q:n * (q + 1), :, :].rearrange("d b h -> b d h"),
                                 x2_s[:, x:x + n, :]).then_inc(x2_out[q % 2], 16)

                def x2_back():
                    x2_write(c - 1, QUARTERS - 1)
                    for i in range(2):
                        after(sp, x2_out[i], 32 * c)
                    after(sp, g_ps, G_GROUPS * (c - 1))
                    sp.dma_start(x2_r[:, :, :],
                                 x2_dram.rearrange("d (b g) h -> (d b) g h", g=G_GROUPS)
                                 ).then_inc(x2_in, 16)

                if mlp:
                    after(sp, dense_ps, c - 2)
                    sp.dma_start(dense_raw[:, :], dense_ctx[bass.ds((c - 2) * P, P), :]).then_inc(dense_in, 16)
                if previous and not layer1:
                    x2_back()
                for half, chunk in ((1, c), (0, c + 1)):
                    if not (layer1 if half == 1 else following):
                        continue
                    if layer1:
                        rep(chunk, half)
                    else:
                        after(sp, x0t_ready, 2)
                    for i in range(PAIR_TILES * half, PAIR_TILES * (half + 1)):
                        pair_tile(chunk, i)
                        if previous and i == X2_LAST_AFTER:
                            x2_back()
                        if layer1 and following and i in X2_WRITES:
                            x2_write(c, X2_WRITES[i])
                if layer1 and not following:
                    for q in range(QUARTERS - 1):
                        x2_write(c, q)

            steps(sp, step)
            for c0, c1 in ((0, CHUNKS - 1), (CHUNKS - 1, CHUNKS)):
                sp.wait_ge(y_ready, c1)
                with nc.allow_non_contiguous_dma(reason="a thousand words off the partitions"):
                    sp.dma_start(y_dram[:, c0:c1], y_sb[:, c0:c1]).then_inc(y_out, 16)
            sp.wait_ge(y_out, 32)
            for i in range(2):
                sp.wait_ge(x2_out[i], 32 * CHUNKS)

        @block.gpsimd
        def _(pool):
            def gather(chunk, f):
                nc.gpsimd.indirect_dma_start(
                    e_in[:, f, :], None, tables[f], bass.IndirectOffsetOnAxis(ap=idx[:, f:f + 1], axis=0)
                ).then_inc(gathered, 16)

            pool.wait_ge(ids_in, 16)
            nc.gpsimd.tensor_copy(idx[:, :], ids_sb[:, 0, :]).then_inc(idx_ready, 1)
            nc.gpsimd.memset(ident[:, :], 0.0).then_inc(zeroed, 1)
            pool.wait_ge(zeroed, 1)
            nc.gpsimd.affine_select(out=ident[:, :], in_=ident[:, :], compare_op=ALU.not_equal, fill=1.0, base=0,
                                    pattern=[[-1, P]], channel_multiplier=1).then_inc(consts_made, 1)
            pool.wait_ge(idx_ready, 1)
            for f in range(FIELDS):
                gather(0, f)

            def step(c, layer1, following, previous, mlp, gathers):
                def next_index():
                    pool.wait_ge(gathered, 16 * FIELDS * (c + 2))
                    nc.gpsimd.tensor_copy(idx[:, :], ids_sb[:, c + 2, :]).then_inc(idx_ready, 1)

                if not layer1:
                    if gathers:
                        next_index()
                        pool.wait_ge(idx_ready, c + 3)
                        pool.wait_ge(e_mid_ready, c + 2)
                        for f in range(FIELDS - LATE):
                            gather(c + 2, f)
                    return
                for d in range(D):
                    t = terms[:, d % 2]
                    n = D * c + d
                    after(pool, act_group, scaled(c, d, GROUPS - 1))
                    after(pool, dve_unit, summed(c, d, DVE_BEFORE[d][GROUPS]))
                    if d % (D // QUARTERS) == 0:
                        q = d // (D // QUARTERS)
                        after(pool, x2_out[q % 2], 32 * c + 16 * (q // 2))
                    for i, terms_left in enumerate(FOLDS[TERMS[d]]):
                        w = terms_left // 2
                        nc.gpsimd.tensor_tensor(t[:, 0:w, :], t[:, 0:w, :], t[:, terms_left - w:terms_left, :],
                                                ALU.add).then_inc(folded, 1)
                        if i == 0 and d == INDEX_SLICE and gathers:
                            next_index()
                            pool.wait_ge(idx_ready, c + 3)
                            pool.wait_ge(e_mid_ready, c + 2)
                        pool.wait_ge(folded, 4 * n + i + 1)
                    nc.gpsimd.tensor_tensor(x2_s[:, d % X2_SLOTS, :], t[:, 0, :], t[:, 1, :],
                                            ALU.add).then_inc(x2_done, 1)
                    if following and d < INDEX_SLICE:
                        for f in range(FIELDS - LATE + sum(GATHERS[:d]), FIELDS - LATE + sum(GATHERS[:d + 1])):
                            gather(c + 1, f)
                    if gathers and d >= INDEX_SLICE:
                        for f in range(sum(GATHERS[INDEX_SLICE:d]), sum(GATHERS[INDEX_SLICE:d + 1])):
                            gather(c + 2, f)

            steps(pool, step)

        @block.scalar
        def _(act):
            def setup_copy(batch, dst, rows, width):
                act.wait_ge(setup_ps, batch + 1)
                nc.scalar.activation(dst, ring[0:rows, batch % RING, 0:width], ACT.Copy).then_inc(setup_hi, 1)

            batch = 0
            for q in range(SETUP_V):
                act.wait_ge(setup_ps, batch + 1)
                for i, t in enumerate(range(4 * q, min(4 * q + 4, PAIR_TILES))):
                    rows = ROWS_OF[t]
                    last = nc.scalar.activation(v_hi[0:rows, t, :], ring[0:rows, batch % RING, i * H:(i + 1) * H],
                                                ACT.Copy)
                last.then_inc(setup_hi, 1)
                batch += 1
            for dst in (w1_hi, w2_t):
                for q in range(GROUPS):
                    n = min(BANK, FIELDS * H - BANK * q)
                    setup_copy(batch, dst[:, BANK * q:BANK * q + n], P, n)
                    batch += 1

            def step(c, layer1, following, previous, mlp, gathers):
                def x1_half(chunk, half):
                    after(act, pair_used, PAIR_TILES * (2 * chunk + half + 1))
                    after(act, y_group, GROUPS * (D * (chunk - 1) + D // 2 * (half + 1)))
                    nc.scalar.activation(x1_hi[:, half * HALF:(half + 1) * HALF], l0_ps[:, :], ACT.Identity,
                                         bias=b0_col[:, 0:1]).then_inc(x1_hi_ready, 1)

                def move_x0(d):
                    if following and d == MOVE_SLICE:
                        after(act, gathered, 16 * FIELDS * (c + 2))
                        after(act, x0t_ps, 4 * (c + 1))
                        after(act, e_cur_ready, c + 1)
                        for i in range(2):
                            last = nc.scalar.activation(e_mid[:, i * FIELDS:(i + 1) * FIELDS, :], e_in[:, :, :],
                                                        ACT.Copy)
                        last.then_inc(e_mid_ready, 1)
                    if d == 1 and previous:
                        after(act, block_made, G_GROUPS * (c - 1))
                        after(act, xb_ready, 2 * c)
                        nc.scalar.activation(xb[1][:, :, :], xb[0][:, :, :], ACT.Copy).then_inc(xb_moved, 1)

                def pair_upper(d, k):
                    made = tiles_made(c, d, layer1, following)
                    if k < len(made) and made[k][1] is not None:
                        chunk, i = made[k]
                        n = TILES * chunk + i
                        rows = ROWS_OF[TILE[i][1]]
                        after(act, pair_made, n + 1)
                        after(act, pair_used, n - 1)
                        nc.scalar.activation(pairs_hi[0:rows, i % 2, :], pair_slot(chunk, i)[0][0:rows, :],
                                             ACT.Copy).then_inc(pair_hi, 1)

                def evacuate_g(chunk, r):
                    for g in (r, r + 1):
                        after(act, g_ps, G_GROUPS * chunk + g + 1)
                        after(act, y_ps, chunk)
                        nc.scalar.activation(
                            g_t[:, :, g::G_GROUPS],
                            side[:, g % 2, 0:SAMPLES_PER_G * GCOLS].rearrange("p (b j) -> p j b", j=GCOLS),
                            ACT.Copy).then_inc(g_ready, 1)

                def side_work(d):
                    e = d - 1
                    if following and e in X0T_SLICES:
                        for q in range(2 * X0T_SLICES.index(e), 2 * X0T_SLICES.index(e) + 2):
                            after(act, x0t_ps, 4 * (c + 1) + q + 1)
                            for s in range(2):
                                if layer1:
                                    after(act, pair_in[s], loads(c + 1, s))
                            after(act, rep_in, 16 * PER_TILE * 2 * (c + 1))
                            after(act, xb_ps, 2 * (c + 1))
                            nc.scalar.activation(x0_t[:, q * BANK:(q + 1) * BANK], side[0:2 * FIELDS, q % 2, :],
                                                 ACT.Copy).then_inc(x0t_ready, 1)
                    if layer1 and e in XB_SLICES:
                        n = G_GROUPS // 2
                        q = XB_SLICES.index(e)
                        after(act, xb_ps, 2 * c + q + 1)
                        after(act, xb_moved, c)
                        nc.scalar.activation(xb[0][:, n * q:n * (q + 1), :], side[:, 1, 0:n * FIELDS],
                                             ACT.Copy).then_inc(xb_ready, 1)
                    if mlp and e < 0:
                        evacuate_g(c - 2, G_GROUPS - 2)
                    if previous and G_FIRST <= e:
                        evacuate_g(c - 1, 2 * (e - G_FIRST))
                    if mlp and e == Z2_SLICES[-1]:
                        after(act, z2_ps, c - 1)
                        nc.scalar.activation(z2_sb, side[:, 0, 0:P], ACT.Identity,
                                             bias=b2_sum[:, 0:1]).then_inc(z2_ready, 1)
                    if mlp and e == DENSE_SLICE:
                        after(act, dense_ps, c - 1)
                        nc.scalar.activation(dense_t, side[0:DENSE, 1, 0:P], ACT.Copy).then_inc(dense_ready, 1)
                    if mlp and e == H1_SLICE:
                        after(act, h1_ps, c - 1)
                        for m in range(M1 // P):
                            last = nc.scalar.activation(h1_sb[:, m, :], side[:, 1, m * P:(m + 1) * P], ACT.Relu,
                                                        bias=btop1[:, m:m + 1])
                        last.then_inc(h1_ready, 1)
                    if mlp and e == H2_SLICE:
                        after(act, h2_ps, c - 1)
                        for m in range(M2 // P):
                            last = nc.scalar.activation(h2_sb[:, m, :], side[:, 0, m * P:(m + 1) * P], ACT.Relu,
                                                        bias=btop2[:, m:m + 1])
                        last.then_inc(h2_ready, 1)
                    if mlp and e == Y_SLICE:
                        after(act, y_ps, c - 1)
                        nc.scalar.activation(y_sb[:, bass.ds(c - 2, 1)], side[:, 1, 0:1], ACT.Copy).then_inc(y_ready, 1)

                for d in range(D):
                    if not layer1:
                        move_x0(d)
                        side_work(d)
                        if following and d == X0T_SLICES[0] + 1:
                            act.wait_ge(x0t_ready, 2)
                            for n in range(PER_TILE):
                                act.dma_start(x0_rep[n * FIELDS:(n + 1) * FIELDS, :],
                                              x0_t[0:FIELDS, 0:HALF]).then_inc(rep_in, 16)
                        for k in range(2):
                            pair_upper(d, k)
                        for half, chunk in halves(c, layer1, following):
                            if d == X1_HI_AT[half][0]:
                                x1_half(chunk, half)
                        continue
                    n = D * c + d
                    if d == 0:
                        act.wait_ge(e_cur_ready, c + 1)
                    after(act, x2_done, n - 1)
                    for g in range(GROUPS):
                        if g == MID:
                            side_work(d)
                        for half, chunk in halves(c, layer1, following):
                            if (d, g) == X1_HI_AT[half]:
                                x1_half(chunk, half)
                        if g == MOVE_MID:
                            move_x0(d)
                        if g in HI_MID:
                            pair_upper(d, HI_MID.index(g))
                        if g not in ACT_GROUPS[d]:
                            continue
                        after(act, y_group, GROUPS * n + g + 1)
                        for i in range(WIDTH[g]):
                            j = GROUP * g + i
                            last = nc.scalar.activation(terms[:, d % 2, ACT_BEFORE[d][g] + i, :],
                                                        ring[:, (GROUPS * d + g) % RING, i * H:(i + 1) * H], ACT.Copy,
                                                        scale=e_cur[:, j, d:d + 1])
                        last.then_inc(act_group, 1)

            act.wait_ge(small_in, 48)
            act.wait_ge(bias_sums, 2)
            act.wait_ge(top_in, 96)
            steps(act, step)

        @block.vector
        def _(dve):
            dve.wait_ge(w0_in, 16)
            nc.vector.tensor_copy(v_raw[:, 0:FIELDS], w0_raw[:, 0:FIELDS * FIELDS:FIELDS + 1])
            for s in range(1, SHIFTS):
                for i0, i1, a, b in ((0, FIELDS - s, s, FIELDS * s),
                                     (FIELDS - s, FIELDS, s - FIELDS, FIELDS * (s - FIELDS))):
                    step40 = FIELDS + 1
                    n = i1 - i0
                    x = step40 * i0 + a
                    y = step40 * i0 + b
                    last = nc.vector.tensor_tensor(
                        v_raw[:, s * FIELDS + i0:s * FIELDS + i1],
                        w0_raw[:, x:x + step40 * (n - 1) + 1:step40],
                        w0_raw[:, y:y + step40 * (n - 1) + 1:step40], ALU.add)
            last.then_inc(v_made, 1)
            dve.wait_ge(small_in, 48)
            nc.vector.tensor_scalar(b0_sum[:, :], b0_col[:, :], float(D), None, ALU.mult).then_inc(bias_sums, 1)
            nc.vector.tensor_scalar(b2_sum[:, :], b2_col[:, :], float(D), None, ALU.mult).then_inc(bias_sums, 1)
            dve.wait_ge(consts_made, 1)
            nc.vector.tensor_reduce(own[:, :], ident[:, :].rearrange("p (d b) -> p b d", d=D), AX.X,
                                    ALU.add).then_inc(own_made, 1)
            dve.wait_ge(own_made, 1)
            for i in range(2):
                nc.vector.tensor_copy(blocks[:, i, :, FIELDS], own[:, :])
            for t in range(PAIR_TILES):
                rows = ROWS_OF[t]
                if t % 4 == 0:
                    dve.wait_ge(setup_hi, t // 4 + 1)
                last = nc.vector.tensor_tensor(v_lo[0:rows, t, :], ring[0:rows, t // 4, t % 4 * H:(t % 4 + 1) * H],
                                               v_hi[0:rows, t, :].bitcast(f32), ALU.subtract)
                if t % 4 == 3 or t == PAIR_TILES - 1:
                    last.then_inc(setup_lo, 1)
            for q in range(GROUPS):
                batch = SETUP_V + q
                n = min(BANK, FIELDS * H - BANK * q)
                dve.wait_ge(setup_hi, batch + 1)
                nc.vector.tensor_tensor(w1_lo[:, BANK * q:BANK * q + n], ring[:, batch % RING, 0:n],
                                        w1_hi[:, BANK * q:BANK * q + n].bitcast(f32),
                                        ALU.subtract).then_inc(setup_lo, 1)

            def step(c, layer1, following, previous, mlp, gathers):
                def x1_lower(chunk, half):
                    x = slice(half * HALF, (half + 1) * HALF)
                    after(dve, x1_hi_ready, 2 * chunk + half + 1)
                    nc.vector.scalar_tensor_tensor(out=x1_lo[:, x], in0=l0_ps[:, :], scalar=b0_col[:, 0:1],
                                                   in1=x1_hi[:, x].bitcast(f32), op0=ALU.add,
                                                   op1=ALU.subtract).then_inc(x1_lo_ready, 1)

                def z0_half(chunk, half):
                    dst = z0_part if half == 0 else z0_new
                    if half == 1 and not (isinstance(chunk, int) and chunk == 0):
                        after(dve, h1_ps, chunk - 1)
                        nc.vector.tensor_copy(z0_old[:, :], z0_new[:, :]).then_inc(z0_kept, 1)
                        dve.wait_ge(z0_kept, chunk)
                    nc.vector.tensor_reduce(dst[:, :], l0_ps[:, :].rearrange("p (d b) -> p b d", b=P),
                                            AX.X, ALU.add).then_inc(z0_summed, 1)
                    if half == 1:
                        after(dve, z0_summed, 2 * chunk + 2)
                        nc.vector.scalar_tensor_tensor(out=z0_new[:, :], in0=z0_part[:, :], scalar=b0_sum[:, 0:1],
                                                       in1=z0_new[:, :], op0=ALU.add,
                                                       op1=ALU.add).then_inc(z0_ready, 1)

                def make_block(d, i):
                    if previous and G_FIRST <= d < G_FIRST + G_GROUPS // 2:
                        g = 2 * (d - G_FIRST) + i
                        if g == 0:
                            after(dve, xb_moved, c)
                        n = G_GROUPS * (c - 1) + g
                        after(dve, g_ps, n - g if g < 2 else n - 1)
                        shape = [P, SAMPLES_PER_G, FIELDS]
                        nc.vector.tensor_tensor(
                            blocks[:, g % 2, :, 0:FIELDS],
                            xb[1][:, g:g + 1, :].to_broadcast(shape),
                            own[:, :].unsqueeze(2).to_broadcast(shape), ALU.mult).then_inc(block_made, 1)

                def side_work(d, g):
                    if g in BLOCK_MID:
                        make_block(d, BLOCK_MID.index(g))
                    for k, (chunk, i) in enumerate(tiles_made(c, d, layer1, following)):
                        if i is not None and g == MADE_MID[k]:
                            half, t = TILE[i]
                            rows = ROWS_OF[t]
                            after(dve, rep_in, 16 * PER_TILE * (2 * chunk + half + 1))
                            products, loaded, count = pair_slot(chunk, i)
                            after(dve, loaded, count)
                            nc.vector.tensor_tensor(products[0:rows, :], x0_rep[0:rows, :], products[0:rows, :],
                                                    ALU.mult).then_inc(pair_made, 1)
                    for k in range(2):
                        slices_later, at = (LO_MID if layer1 else LO_MID_FIRST)[k]
                        made = tiles_made(c, d - slices_later, layer1, following)
                        if g == at and k < len(made) and made[k][1] is not None:
                            chunk, i = made[k]
                            n = TILES * chunk + i
                            rows = ROWS_OF[TILE[i][1]]
                            after(dve, pair_hi, n + 1)
                            after(dve, pair_used, n - 1)
                            nc.vector.tensor_tensor(pairs_lo[0:rows, i % 2, :], pair_slot(chunk, i)[0][0:rows, :],
                                                    pairs_hi[0:rows, i % 2, :].bitcast(f32),
                                                    ALU.subtract).then_inc(pair_lo, 1)
                    for half, chunk in halves(c, layer1, following):
                        if (d, g) == X1_LO_AT[half]:
                            x1_lower(chunk, half)
                        if (d, g) == Z0_AT[half]:
                            z0_half(chunk, half)

                if layer1:
                    after(dve, act_group, scaled(c, -1, GROUPS - 1))
                    after(dve, dve_unit, summed(c, 0, 0))
                    after(dve, e_mid_ready, c + 1)
                    nc.vector.tensor_copy(e_cur[:, :, :], e_mid[:, 0:FIELDS, :]).then_inc(e_cur_ready, 1)
                    dve.wait_ge(e_cur_ready, c + 1)
                for d in range(D):
                    n = D * c + d
                    if layer1:
                        after(dve, x2_done, n - 1)
                    unit = 0
                    for g in range(GROUPS):
                        side_work(d, g)
                        if not layer1:
                            continue
                        if g in ACT_GROUPS[d]:
                            continue
                        after(dve, y_group, GROUPS * n + g + 1)
                        for i in range(WIDTH[g]):
                            j = GROUP * g + i
                            y = ring[:, (GROUPS * d + g) % RING, i * H:(i + 1) * H]
                            acc = terms[:, d % 2, TERMS[d] - 2 + unit % 2, :]
                            if unit == 0:
                                nc.vector.scalar_tensor_tensor(out=acc, in0=y, scalar=e_cur[:, j, d:d + 1],
                                                               in1=b1_rows[:, :], op0=ALU.mult,
                                                               op1=ALU.add).then_inc(dve_unit, 1)
                            elif unit == 1:
                                nc.vector.tensor_scalar(acc, y, e_cur[:, j, d:d + 1], None,
                                                        ALU.mult).then_inc(dve_unit, 1)
                            else:
                                after(dve, dve_unit, summed(c, d, unit - 1))
                                nc.vector.scalar_tensor_tensor(out=acc, in0=y, scalar=e_cur[:, j, d:d + 1],
                                                               in1=acc, op0=ALU.mult,
                                                               op1=ALU.add).then_inc(dve_unit, 1)
                            unit += 1

            steps(dve, step)

        @block.tensor
        def _(pe):
            pe.wait_ge(consts_made, 1)
            batch = 0

            def bank_free(batch):
                after(pe, setup_hi, batch - RING + 1)
                after(pe, setup_lo, min(batch - RING + 1, SETUP_V + SETUP_W1))

            pe.wait_ge(v_made, 1)
            for q in range(SETUP_V):
                bank_free(batch)
                for i, t in enumerate(range(4 * q, min(4 * q + 4, PAIR_TILES))):
                    x = PER_TILE * FIELDS * t
                    rows = ROWS_OF[t]
                    last = nc.tensor.transpose(ring[0:rows, batch % RING, i * H:(i + 1) * H], v_raw[:, x:x + rows],
                                               ident[:, :])
                last.then_inc(setup_ps, 1)
                batch += 1
            for loaded in (w1_in, w2_in):
                pe.wait_ge(loaded, 16)
                for q in range(GROUPS):
                    bank_free(batch)
                    for i, j in enumerate(range(GROUP * q, min(GROUP * (q + 1), FIELDS))):
                        last = nc.tensor.transpose(ring[:, batch % RING, i * H:(i + 1) * H],
                                                   w12_raw[:, j * H:(j + 1) * H], ident[:, :])
                    last.then_inc(setup_ps, 1)
                    batch += 1

            def step(c, layer1, following, previous, mlp, gathers):
                def layer0(chunk, i, x):
                    half, t = TILE[i]
                    rows = ROWS_OF[t]
                    n = 2 * chunk + half
                    if x == 0:
                        if t == 0:
                            after(pe, x1_hi_ready, n)
                            after(pe, x1_lo_ready, n)
                            after(pe, z0_summed, n)
                        after(pe, pair_lo, TILES * chunk + i + 1)
                    p_hi, p_lo = pairs_hi[0:rows, i % 2, x:x + BANK], pairs_lo[0:rows, i % 2, x:x + BANK]
                    acc = l0_ps[:, x:x + BANK]
                    nc.tensor.matmul(acc, v_hi[0:rows, t, :], p_hi, start=(t == 0), stop=False)
                    nc.tensor.matmul(acc, v_lo[0:rows, t, :], p_hi, start=False, stop=False)
                    last = nc.tensor.matmul(acc, v_hi[0:rows, t, :], p_lo, start=False, stop=(t == PAIR_TILES - 1))
                    if x:
                        last.then_inc(pair_used, 1)

                def side_work(d, g):
                    if mlp and d in Z2_SLICES:
                        j0 = Z2_AT_ONCE * (GROUPS * Z2_SLICES.index(d) + g - Z2_FROM)
                        if j0 == 0:
                            after(pe, g_ready, G_GROUPS * (c - 1))
                        for j in range(max(j0, 0), min(j0 + Z2_AT_ONCE, FIELDS)):
                            last = nc.tensor.matmul(side[:, 0, 0:P], w2_t[:, j * H:(j + 1) * H], g_t[:, j, :],
                                                    start=(j == 0), stop=(j == FIELDS - 1))
                            if j == FIELDS - 1:
                                last.then_inc(z2_ps, 1)
                    if layer1 and d in XB_SLICES and g == XB_AT:
                        q = XB_SLICES.index(d)
                        n = G_GROUPS // 2
                        for i in range(n):
                            r = q * n + i
                            last = nc.tensor.transpose(side[:, 1, i * FIELDS:(i + 1) * FIELDS],
                                                       x0_t[0:FIELDS, r::G_GROUPS],
                                                       ident[0:FIELDS, 0:FIELDS])
                        last.then_inc(xb_ps, 1)
                    if mlp and d == DENSE_SLICE and g == GROUPS - 1:
                        after(pe, dense_in, 16 * (c - 1))
                        if layer1:
                            after(pe, xb_ready, 2 * (c + 1))
                        nc.tensor.transpose(side[0:DENSE, 1, 0:P], dense_raw[:, :], ident[:, :]).then_inc(dense_ps, 1)
                    if mlp and d == H1_SLICE and g in H1_AT:
                        m = H1_AT.index(g)
                        last_chunk = isinstance(c, int) and c == CHUNKS + 1
                        if m == 0:
                            after(pe, z2_ready, c - 1)
                            after(pe, z0_ready, c - 1)
                            after(pe, dense_ready, c - 1)
                            if not last_chunk:
                                after(pe, z0_kept, c - 1)
                        z0 = z0_new if last_chunk else z0_old
                        for k, z in enumerate((z0[:, :], g_t[:, FIELDS, :], z2_sb, dense_t)):
                            rows = DENSE if k == 3 else P
                            last = nc.tensor.matmul(side[:, 1, m * P:(m + 1) * P],
                                                    wtop1[0:rows, k, m * P:(m + 1) * P], z,
                                                    start=(k == 0), stop=(k == 3))
                        if m == M1 // P - 1:
                            last.then_inc(h1_ps, 1)
                    if mlp and d == H2_SLICE and g in TWO_AT:
                        after(pe, h1_ready, c - 1)
                        m = TWO_AT.index(g)
                        for k in range(M1 // P):
                            last = nc.tensor.matmul(side[:, 0, m * P:(m + 1) * P],
                                                    wtop2[:, k, m * P:(m + 1) * P], h1_sb[:, k, :],
                                                    start=(k == 0), stop=(k == M1 // P - 1))
                        if m == M2 // P - 1:
                            last.then_inc(h2_ps, 1)
                    if mlp and d == Y_SLICE and g == Y_AT:
                        after(pe, h2_ready, c - 1)
                        for k in range(M2 // P):
                            last = nc.tensor.matmul(side[:, 1, 0:1], h2_sb[:, k, :], wtop3[:, k:k + 1],
                                                    start=(k == 0), stop=(k == M2 // P - 1))
                        last.then_inc(y_ps, 1)
                    if following and d in X0T_SLICES and g in TWO_AT:
                        q = 2 * X0T_SLICES.index(d) + TWO_AT.index(g)
                        if q == 0:
                            after(pe, h2_ready, c - 1)
                            after(pe, y_ready, c - 1)
                            after(pe, xb_ready, 2 * (c + 1))
                            after(pe, g_ready, G_GROUPS * (c - 1))
                            after(pe, e_mid_ready, c + 2)
                        after(pe, x0t_ready, 4 * (c + 1) + q - 1)
                        for i in range(4):
                            last = nc.tensor.transpose(side[0:2 * FIELDS, q % 2, i * P:(i + 1) * P],
                                                       e_mid[:, :, 4 * q + i], ident[:, :])
                        last.then_inc(x0t_ps, 1)
                    if previous and G_FIRST <= d and g in TWO_AT:
                        r = 2 * (d - G_FIRST) + TWO_AT.index(g)
                        if r == 0:
                            if following:
                                after(pe, x0t_ready, 4 * (c + 2))
                            elif layer1:
                                after(pe, xb_ready, 2 * (c + 1))
                            after(pe, h2_ready, c - 1)
                            after(pe, y_ready, c - 1)
                            after(pe, x2_in, 16 * c)
                        n = G_GROUPS * (c - 1) + r
                        after(pe, block_made, n + 1)
                        if r >= 2:
                            after(pe, g_ready, n - 1)
                        nc.tensor.matmul(side[:, r % 2, 0:SAMPLES_PER_G * GCOLS], x2_r[:, r, :],
                                         blocks[:, r % 2, :, :].rearrange("p b j -> p (b j)"),
                                         start=True, stop=True).then_inc(g_ps, 1)
                    for (chunk, i), at in zip(tiles_made(c, d - 1, layer1, following), L0_AT):
                        if i is not None and g in at:
                            layer0(chunk, i, at.index(g) * BANK)

                for d in range(D):
                    if layer1 and d % (D // 2) == 0:
                        k = 2 * c + d // (D // 2) + 1
                        after(pe, x1_hi_ready, k)
                        after(pe, x1_lo_ready, k)
                    x = slice(d * P, (d + 1) * P)
                    for g in range(GROUPS):
                        if layer1:
                            width = WIDTH[g] * H
                            w = slice(g * BANK, g * BANK + width)
                            if d in XB_SLICES and g == XB_AT:
                                after(pe, x0t_ready, 4 * (c + 1))
                                after(pe, xb_ready, 2 * c + XB_SLICES.index(d))
                                if mlp:
                                    after(pe, g_ready, G_GROUPS * (c - 1))
                            e, b = (d, g - RING) if g >= RING else (d - 1, g - RING + GROUPS)
                            if b in ACT_GROUPS[e]:
                                after(pe, act_group, scaled(c, e, b))
                            else:
                                after(pe, dve_unit, summed(c, e, DVE_BEFORE[e][b + 1]))
                            acc = ring[:, (GROUPS * d + g) % RING, 0:width]
                            nc.tensor.matmul(acc, x1_hi[:, x], w1_hi[:, w], start=True, stop=False)
                            nc.tensor.matmul(acc, x1_hi[:, x], w1_lo[:, w], start=False, stop=False)
                            nc.tensor.matmul(acc, x1_lo[:, x], w1_hi[:, w], start=False,
                                             stop=True).then_inc(y_group, 1)
                        side_work(d, g)

            pe.wait_ge(top_in, 96)
            pe.wait_ge(setup_hi, SETUP)
            pe.wait_ge(setup_lo, SETUP_V + SETUP_W1)
            steps(pe, step)


_TABLES = [f"tbl_{f}" for f in range(TABLES)]
_INS = (["dense_ctx", "ids"] + _TABLES + ["W_top1", "b_top1", "W_top2", "b_top2", "W_top3"]
        + [f"L0_rec_{kind}{layer}" for layer in range(3) for kind in "Wb"])


def kernel(**inputs):
    import numpy as _np
    import concourse.bacc as _bacc
    from concourse import mybir as _mybir
    from concourse.bass_utils import run_bass_kernel_spmd as _run

    nc = _bacc.Bacc("TRN2", target_bir_lowering=False, num_devices=1)
    arrays, aps = {}, {}
    for name in _INS:
        a = _np.ascontiguousarray(inputs[name])
        arrays[f"in_{name}"] = a
        aps[name] = nc.dram_tensor(f"in_{name}", a.shape, _mybir.dt.from_np(a.dtype), kind="ExternalInput").ap()
    batch = arrays["in_ids"].shape[0]
    out = nc.dram_tensor("out_y", (batch, 1), _mybir.dt.float32, kind="ExternalOutput").ap()
    build_tower(nc, aps["dense_ctx"], aps["ids"], [aps[t] for t in _TABLES], aps["W_top1"], aps["b_top1"],
                aps["W_top2"], aps["b_top2"], aps["W_top3"], aps["L0_rec_W0"], aps["L0_rec_b0"], aps["L0_rec_W1"],
                aps["L0_rec_b1"], aps["L0_rec_W2"], aps["L0_rec_b2"], out)
    return _run(nc, [arrays], core_ids=[0]).results[0]["out_y"]
```
